# Optimizing a Trainium2 kernel written in Bass

```python
import numpy as np
import jax
import jax.numpy as jnp

def _softmax(x, axis=-1):
    return jax.nn.softmax(x, axis=axis)

def _gelu(x):
    return jax.nn.gelu(x, approximate=True)

def _silu(x):
    return jax.nn.silu(x)

def _sigmoid(x):
    return jax.nn.sigmoid(x)

def _layernorm(x, axis=-1, eps=1e-05):
    m = jnp.mean(x, axis=axis, keepdims=True)
    v = jnp.var(x, axis=axis, keepdims=True)
    return (x - m) / jnp.sqrt(v + eps)

def _scatter_add(tgt, idx, src, axis=0):
    return tgt.at[idx].add(src)

def _segment_sum(src, seg, n):
    return jax.ops.segment_sum(src, seg, n)
kernel_name = 'mk_flamingo_gated_d1_seqx_r4_7ca89f'

def setup_inputs(seed: int=0):
    np.random.seed(seed)
    _w = jnp.asarray

    def _rec_inputs():
        import jax
        import jax.numpy as jnp
        _rk = jax.random.key(seed)
        x = 7.22e-05 + 1 * jax.random.normal(jax.random.fold_in(_rk, 1), (1, 2048, 256), jnp.float32)
        _lenS = 2048 - jax.random.randint(jax.random.fold_in(_rk, 7), (1,), 0, max(1, 2048 // 4) + 1, jnp.int32)
        _lenS2 = 1601 - jax.random.randint(jax.random.fold_in(_rk, 8), (1,), 0, max(1, 1601 // 4) + 1, jnp.int32)
        _ctx_1024P = jax.random.normal(jax.random.fold_in(_rk, 11), (1, 16, 256), jnp.float32)
        _ctx_1024c = jax.random.dirichlet(jax.random.fold_in(_rk, 511), 0.3 * jnp.ones((16,), jnp.float32), (1, 1601))
        _ctx_1024t = jnp.einsum('bsk,bkd->bsd', _ctx_1024c, _ctx_1024P)
        _ctx_1024t = _ctx_1024t * jax.lax.rsqrt(jnp.mean(jnp.square(_ctx_1024t)) + 1e-12) * 0.953939
        ctx_1024 = 4.13588e-05 + 0.999923 * (_ctx_1024t + 0.3 * jax.random.normal(jax.random.fold_in(_rk, 611), (1, 1601, 256), jnp.float32))
        _g = jax.random.normal(jax.random.fold_in(_rk, 9001), (2, 1), jnp.float32)
        _g = jnp.sign(_g) * jnp.maximum(jnp.abs(_g), 1.0) + (_g == 0) * 1.0
        g_xattn = _g[0]
        g_ffn = _g[1]
        return (x, ctx_1024, g_xattn, g_ffn)
    x, ctx_1024, g_xattn, g_ffn = _rec_inputs()

    def _L0_xattn_setup():
        import jax, jax.numpy as jnp
        import numpy as np
        C = 256
        B, SQ, SKV = (4, 512, 512)
        key = jax.random.key(seed)
        ks = jax.random.split(key, 10)
        s = 1.0 / np.sqrt(C)
        return {'x': jax.random.normal(ks[0], (B, SQ, C), jnp.float32), 'content_embeddings': jax.random.normal(ks[1], (B, SKV, C), jnp.float32), 'Wq': jax.random.normal(ks[2], (C, C), jnp.float32) * s, 'bq': jnp.zeros((C,), jnp.float32), 'Wk': jax.random.normal(ks[3], (C, C), jnp.float32) * s, 'bk': jnp.zeros((C,), jnp.float32), 'Wv': jax.random.normal(ks[4], (C, C), jnp.float32) * s, 'bv': jnp.zeros((C,), jnp.float32), 'Wo': jax.random.normal(ks[5], (C, C), jnp.float32) * s, 'bo': jnp.zeros((C,), jnp.float32)}
    _L0_xattn_all = _L0_xattn_setup()
    _L0_xattn_in = {k: v for k, v in _L0_xattn_all.items() if k in ('Wq', 'bq', 'Wk', 'bk', 'Wv', 'bv', 'Wo', 'bo')}
    del _L0_xattn_all

    def _L0_ffn_setup():
        import jax, jax.numpy as jnp
        import numpy as np
        E = 8
        K = 2
        R = 64
        ALPHA = 128.0
        SCALING = ALPHA / R
        key = jax.random.key(seed)
        k0, k1, k2, k3 = jax.random.split(key, 4)
        B, S, D = (4, 1024, 256)
        x = jax.random.normal(k0, (B, S, D), jnp.float32)
        Wg = jax.random.normal(k1, (E, D), jnp.float32) * 0.02
        bg = jnp.zeros((E,), jnp.float32)
        W1 = jax.random.normal(k2, (E, R, D), jnp.float32) * (1.0 / np.sqrt(D))
        W2 = jax.random.normal(k3, (E, D, R), jnp.float32) * 0.02
        return {'x': x, 'Wg': Wg, 'bg': bg, 'W1': W1, 'W2': W2}
    _L0_ffn_all = _L0_ffn_setup()
    _L0_ffn_in = {k: v for k, v in _L0_ffn_all.items() if k in ('Wg', 'bg', 'W1', 'W2')}
    del _L0_ffn_all
    return {'x': x, 'ctx_1024': ctx_1024, 'g_xattn': g_xattn, 'g_ffn': g_ffn, 'L0_xattn_Wq': _L0_xattn_in['Wq'], 'L0_xattn_bq': _L0_xattn_in['bq'], 'L0_xattn_Wk': _L0_xattn_in['Wk'], 'L0_xattn_bk': _L0_xattn_in['bk'], 'L0_xattn_Wv': _L0_xattn_in['Wv'], 'L0_xattn_bv': _L0_xattn_in['bv'], 'L0_xattn_Wo': _L0_xattn_in['Wo'], 'L0_xattn_bo': _L0_xattn_in['bo'], 'L0_ffn_Wg': _L0_ffn_in['Wg'], 'L0_ffn_bg': _L0_ffn_in['bg'], 'L0_ffn_W1': _L0_ffn_in['W1'], 'L0_ffn_W2': _L0_ffn_in['W2']}

def reference(x, ctx_1024, g_xattn, g_ffn, L0_xattn_Wq, L0_xattn_bq, L0_xattn_Wk, L0_xattn_bk, L0_xattn_Wv, L0_xattn_bv, L0_xattn_Wo, L0_xattn_bo, L0_ffn_Wg, L0_ffn_bg, L0_ffn_W1, L0_ffn_W2):
    import jax
    import jax.numpy as jnp

    def _L0_xattn_ref(x, content_embeddings, Wq, bq, Wk, bk, Wv, bv, Wo, bo):
        import jax, jax.numpy as jnp
        import numpy as np
        C = 256
        B, SQ, SKV = (4, 512, 512)
        queries = x @ Wq.T + bq
        keys = content_embeddings @ Wk.T + bk
        values = content_embeddings @ Wv.T + bv
        scale = 1.0 / jnp.sqrt(jnp.asarray(C, x.dtype))
        scores = jnp.einsum('bqc,bkc->bqk', queries, keys) * scale
        attn = jax.nn.softmax(scores, axis=-1)
        attended = jnp.einsum('bqk,bkc->bqc', attn, values)
        out = x + attended
        return out @ Wo.T + bo

    def _L0_ffn_ref(x, Wg, bg, W1, W2):
        import jax, jax.numpy as jnp
        import numpy as np
        E = 8
        K = 2
        R = 64
        ALPHA = 128.0
        SCALING = ALPHA / R
        orig_shape = x.shape
        D = orig_shape[-1]
        xf = x.reshape(-1, D)
        logits = xf @ Wg.T + bg
        top_gates, top_idx = jax.lax.top_k(logits, K)
        top_gates = jax.nn.softmax(top_gates, axis=-1)
        h = jax.nn.gelu(jnp.einsum('nd,erd->enr', xf, W1), approximate=False)
        eout = SCALING * jnp.einsum('enr,edr->ned', h, W2)
        sel = jnp.take_along_axis(eout, top_idx[:, :, None], axis=1)
        out = jnp.sum(top_gates[:, :, None] * sel, axis=1)
        return out.reshape(orig_shape)
    x = x + jnp.tanh(g_xattn[0]) * _L0_xattn_ref(_layernorm(x, axis=-1), ctx_1024, L0_xattn_Wq, L0_xattn_bq, L0_xattn_Wk, L0_xattn_bk, L0_xattn_Wv, L0_xattn_bv, L0_xattn_Wo, L0_xattn_bo)
    x = x + jnp.tanh(g_ffn[0]) * _L0_ffn_ref(_layernorm(x, axis=-1), L0_ffn_Wg, L0_ffn_bg, L0_ffn_W1, L0_ffn_W2)
    return x

_drawn_inputs = setup_inputs


def setup_inputs(seed=0):
    import zlib

    import numpy as np

    out = dict(_drawn_inputs(seed))
    spreads = {'L0_xattn_bq': (0.0, 0.528),
     'L0_xattn_bk': (0.0, 0.8),
     'L0_xattn_bv': (0.0, 0.1),
     'L0_xattn_bo': (0.0, 0.1),
     'L0_ffn_bg': (0.0, 0.1)}
    factors = {}
    for name, (base, spread) in spreads.items():
        noise = np.random.default_rng([zlib.crc32(name.encode()), seed]).standard_normal(out[name].shape)
        drawn = base * np.exp(spread * noise) if base else spread * noise
        out[name] = jnp.asarray(drawn.astype(out[name].dtype))
    for name, factor in factors.items():
        out[name] = (out[name] * factor).astype(out[name].dtype)
    return out
```

```python
from contextlib import ExitStack

import concourse.bass as bass
from concourse import mybir

ALU = mybir.AluOpType
ACT = mybir.ActivationFunctionType
AX_X = mybir.AxisListType.X
F32 = mybir.dt.float32
F32R = mybir.dt.float32r
U32 = mybir.dt.uint32

P = 128
EPS = 1e-5
LORA_SCALING = 2.0


def flamingo_layer(nc, x, ctx_1024, g_xattn, g_ffn, Wq, bq, Wk, bk, Wv, bv, Wo, bo, Wg, bg, W1, W2, out):
    SQ, D = x.shape[1], x.shape[2]
    KEYS = ctx_1024.shape[1]
    E, R, _ = W1.shape
    TILES = SQ // P
    DC = D // P
    FULL = KEYS // P
    REST = KEYS - FULL * P
    KT = FULL + 1
    KPAD = KEYS + KEYS % 2
    CH = 402
    CHUNKS = [(c * CH, min(CH, KPAD - c * CH)) for c in range(4)]
    GROUPS = [range(g * 4, min(g * 4 + 4, KT)) for g in range(4)]
    HALF = 2 * CH
    ER = E * R
    ET = ER // P
    UPW = ER // 2 + E // 2
    SCALE = float(D) ** -0.5
    assert D == 2 * P and REST > 0 and CHUNKS[-1][0] + CHUNKS[-1][1] == KPAD and ER == 512
    assert TILES % 2 == 0 and TILES >= 8

    with ExitStack() as ctx:
        def sb(name, shape, dt=F32):
            return ctx.enter_context(nc.sbuf_tensor(name, shape, dt))

        def bank(name):
            return ctx.enter_context(nc.psum_tensor(name, [P, 512], F32))

        def sem(name):
            return ctx.enter_context(nc.semaphore(name))

        X = sb("X", [P, TILES * D])
        ident = sb("ident", [P, P])
        ctx_nat = sb("ctx_nat", [P, KT, D])
        ctxT_hi = sb("ctxT_hi", [P, DC, KPAD], F32R)
        ctxT_lo = sb("ctxT_lo", [P, DC, KPAD], F32R)
        wq = sb("wq", [P, DC, D])
        wk = sb("wk", [P, DC, D])
        wv = sb("wv", [P, DC, D])
        wo = sb("wo", [P, DC, D])
        woT = sb("woT", [P, DC, D])
        woT_hi = sb("woT_hi", [P, DC, D], F32R)
        woT_lo = sb("woT_lo", [P, DC, D], F32R)
        wkq_hi = sb("wkq_hi", [P, DC, D], F32R)
        wkq_lo = sb("wkq_lo", [P, DC, D], F32R)
        wvo_hi = sb("wvo_hi", [P, DC, D], F32R)
        wvo_lo = sb("wvo_lo", [P, DC, D], F32R)
        KQ_hi = sb("KQ_hi", [P, DC, KPAD], F32R)
        KQ_lo = sb("KQ_lo", [P, DC, KPAD], F32R)
        VO_sum = sb("VO_sum", [P, 2, D])
        VO_hi = sb("VO_hi", [P, KT, D], F32R)
        VO_lo = sb("VO_lo", [P, KT, D], F32R)
        key_bias = sb("key_bias", [P, KPAD])
        bq_col = sb("bq_col", [P, DC])
        bk_col = sb("bk_col", [P, DC])
        bv_col = sb("bv_col", [P, DC])
        bo_row = sb("bo_row", [1, D])
        bq_wide = sb("bq_wide", [P, DC, P])
        bv_wide = sb("bv_wide", [P, DC, P])
        ones_row = sb("ones_row", [1, P])
        small = sb("small", [P, 8])
        bqwk_hi = sb("bqwk_hi", [P, DC, P], F32R)
        bqwk_lo = sb("bqwk_lo", [P, DC, P], F32R)
        vo_bias = sb("vo_bias", [P, D])
        gates = sb("gates", [P, 2])
        gate_tanh = sb("gate_tanh", [P, 2])
        ffn_scale = sb("ffn_scale", [P, 1])
        x_bn = sb("x_bn", [P, 2, 6])
        x_mv = sb("x_mv", [P, 2, 2])
        x_ve = sb("x_ve", [P, 2])
        x_rstd = sb("x_rstd", [P, 2])
        x_shift = sb("x_shift", [P, 2])
        minus_half = sb("minus_half", [P, TILES])
        xn = sb("xn", [P, 2, D])
        xnT_hi = sb("xnT_hi", [P, 2, DC, P], F32R)
        xnT_lo = sb("xnT_lo", [P, 2, DC, P], F32R)
        probs = sb("probs", [P, 2, KPAD])
        chunk_max = sb("chunk_max", [P, 2, 4])
        row_max = sb("row_max", [P, 2])
        exp_bias = sb("exp_bias", [P, 2])
        half_sum = sb("half_sum", [P, 2, 2])
        row_sum = sb("row_sum", [P, 1])
        row_inv = sb("row_inv", [P, 1])
        row_gain = sb("row_gain", [P, 1])
        pT_hi = sb("pT_hi", [P, KT, P], F32R)
        pT_lo = sb("pT_lo", [P, KT, P], F32R)
        resid = sb("resid", [P, D])
        z_bn = sb("z_bn", [P, 6])
        z_mv = sb("z_mv", [P, 2, 2])
        z_all = sb("z_all", [P, TILES * 2])
        z_ve = sb("z_ve", [P, TILES])
        z_rstd = sb("z_rstd", [P, TILES])
        z_negm = sb("z_negm", [P, TILES])
        z_shift = sb("z_shift", [P, TILES])
        w1 = sb("w1", [P, ET, D])
        w2 = sb("w2", [P, DC, E, R])
        wg = sb("wg", [E, D])
        bg_wide = sb("bg_wide", [P, E])
        w2T_hi = sb("w2T_hi", [P, ET, D], F32R)
        w2T_lo = sb("w2T_lo", [P, ET, D], F32R)
        ctx_flat = ctx_nat[:].rearrange("p n d -> p (n d)")
        hid = ctx_flat[:, 0:2 * ER].rearrange("p (b e r) -> p b e r", b=2, e=E)
        zb = ctx_flat[:, 2 * ER:2 * ER + 2 * D].rearrange("p (b d) -> p b d", b=2)

        def reuse(w):
            flat, a, b = w[:].rearrange("p a k -> p (a k)"), DC * 2 * UPW, 2 * ER
            return (flat[:, 0:a].rearrange("p (a b n) -> p a b n", a=DC, b=2),
                    flat[:, a:a + b].rearrange("p (b a n) -> p b a n", b=2, a=ET),
                    flat[:, a + b:a + b + 2 * D].rearrange("p (b a n) -> p b a n", b=2, a=DC))

        w1T_hi, hT_hi, zT_hi = reuse(ctxT_hi)
        w1T_lo, hT_lo, zT_lo = reuse(ctxT_lo)
        logits = sb("logits", [P, 2, E])
        top8 = sb("top8", [P, 2, 8])
        top_idx = sb("top_idx", [P, 2, 8], U32)
        top_diff = sb("top_diff", [P, 2])
        top_tanh = sb("top_tanh", [P, 2])
        top_gate = sb("top_gate", [P, 2, 2])
        expert_no = sb("expert_no", [P, E])
        half_signs = sb("half_signs", [P, 2])
        halves = sb("halves", [P, 2])
        is_top = sb("is_top", [P, 2, 2, E])
        gate_two = sb("gate_two", [P, 2, 2, E])
        expert_gate = sb("expert_gate", [P, 2, E])

        S = [bank(f"S{c}") for c in range(4)]
        T = [bank(f"T{c}") for c in range(2)]
        A = bank("A")
        B = bank("B")

        ld = {n: sem("ld_" + n) for n in ("wkq", "bkq", "ctx0", "ctx1", "ctx2", "wo", "wv", "bvo", "gates",
                                          "x0", "x1", "w1", "w2", "wg")}
        s_ident0 = sem("ident_zero"); s_ident = sem("ident_ready")
        s_const = sem("constants_ready")
        s_gate = sem("gate_tanh_ready"); s_fscale = sem("ffn_scale_ready")
        s_wide = sem("wide_biases_ready")
        s_wkq_mm = sem("wkq_product"); s_wkq_hi = sem("wkq_hi_ready"); s_wkq_lo = sem("wkq_lo_ready")
        s_small_mm = sem("small_products"); s_small = sem("small_ready")
        s_bqwk_hi = sem("bqwk_hi_ready"); s_bqwk = sem("bqwk_ready")
        s_cT = sem("ctx_transposed"); s_cT_hi = sem("ctxT_hi_ready"); s_cT_lo = sem("ctxT_lo_ready")
        s_pad = sem("ctxT_pad_zero")
        s_kq_mm = sem("KQ_product"); s_kq_hi = sem("KQ_hi_ready"); s_kq_lo = sem("KQ_lo_ready")
        s_kb_mm = sem("key_bias_product"); s_kb = sem("key_bias_ready")
        s_woT_mm = sem("wo_transposed"); s_woT = sem("woT_ready"); s_woT_hi = sem("woT_hi_ready")
        s_woT_lo = sem("woT_lo_ready")
        s_wvo_mm = sem("wvo_product"); s_wvo_hi = sem("wvo_hi_ready"); s_wvo_lo = sem("wvo_lo_ready")
        s_vb_mm = sem("vo_bias_product"); s_vb = sem("vo_bias_ready")
        s_vo_mm = sem("VO_product"); s_vo_sum = sem("VO_sum_ready"); s_vo_hi = sem("VO_hi_ready")
        s_vo_lo = sem("VO_lo_ready")
        s_xbn = sem("x_bn_ready"); s_xmv = sem("x_mv_ready"); s_xve = sem("x_ve_ready")
        s_xpow = sem("x_rstd_ready"); s_xsh = sem("x_shift_ready")
        s_xn = sem("xn_ready"); s_xnT = sem("xn_transposed"); s_xnT_hi = sem("xnT_hi_ready")
        s_xnT_lo = sem("xnT_lo_ready")
        s_score = sem("scores_product"); s_biased = sem("scores_biased"); s_max = sem("row_max_ready")
        s_ebias = sem("exp_bias_ready"); s_exp = sem("probs_ready")
        s_pT = sem("probs_transposed"); s_pT_hi = sem("pT_hi_ready"); s_pT_lo = sem("pT_lo_ready")
        s_sum = sem("row_sum_ready"); s_inv = sem("row_inv_ready"); s_gain = sem("row_gain_ready")
        s_attn = sem("attention_product"); s_resid = sem("resid_ready"); s_x1 = sem("x1_ready")
        s_zbn = sem("z_bn_ready"); s_zmv = sem("z_mv_ready"); s_zall = sem("z_statistics_kept")
        s_w1T_mm = sem("w1_transposed"); s_w1T_hi = sem("w1T_hi_ready"); s_w1T_lo = sem("w1T_lo_ready")
        s_wgT_mm = sem("wg_transposed"); s_wgT_hi = sem("wgT_hi_ready"); s_wgT_lo = sem("wgT_lo_ready")
        s_w2T_mm = sem("w2_transposed"); s_w2T_hi = sem("w2T_hi_ready"); s_w2T_lo = sem("w2T_lo_ready")
        s_zve = sem("z_ve_ready"); s_zpow = sem("z_rstd_ready"); s_zneg = sem("z_negm_ready")
        s_zsh = sem("z_shift_ready")
        s_z = sem("z_ready"); s_zT = sem("z_transposed"); s_zT_hi = sem("zT_hi_ready")
        s_zT_lo = sem("zT_lo_ready")
        s_up = sem("up_product"); s_logit2 = sem("first_logits_ready"); s_logit = sem("last_logits_ready"); s_top = sem("top8_ready")
        s_idx = sem("top_idx_ready"); s_diff = sem("top_diff_ready"); s_ttanh = sem("top_tanh_ready")
        s_tgate = sem("top_gate_ready"); s_is = sem("is_top_ready"); s_two = sem("gate_two_ready")
        s_eg = sem("expert_gate_ready")
        s_gelu = sem("gelu_ready"); s_gated = sem("hidden_gated")
        s_hT = sem("hidden_transposed"); s_hT_hi = sem("hT_hi_ready"); s_hT_lo = sem("hT_lo_ready")
        s_down = sem("down_product"); s_final = sem("final_ready"); s_out = sem("out_stored")

        def f32(ap):
            return ap.bitcast(F32)

        def count(eng, value):
            return value if isinstance(value, int) else eng.compute_val(value)

        def tile_of(t):
            return X[:, bass.ds(t * D, D)]

        def key_rows(n):
            return P if n < FULL else REST

        def ctxT_part(dst, g):
            n = 2 * P if g < 6 else REST
            return (dst[:, :, g * 2 * P:g * 2 * P + n],
                    S[g % 4][:].rearrange("p (a k) -> p a k", a=2)[:, :, 0:n])

        def pT_part(dst, g):
            tiles = GROUPS[g]
            rows = key_rows(tiles[-1])
            n = len(tiles)
            return (rows, dst[0:rows, tiles[0]:tiles[0] + n, :].rearrange("p a d -> p (a d)"),
                    T[g % 2][0:rows, 0:n * P])

        def wgT_part():
            return B[:, 0:DC * E].rearrange("p (a b n) -> p a b n", a=DC, b=2)

        block = ctx.enter_context(nc.Block())

        x_rows = x[0].rearrange("(p t) d -> p (t d)", t=TILES)
        out_rows = out[0].rearrange("(p t) d -> p (t d)", t=TILES)

        @block.sync
        def _(sp):
            full = ctx_1024[0, 0:FULL * P, :].rearrange("(p n) d -> p n d", n=FULL)
            h = FULL // 2
            sp.dma_start(wk[:], Wk.rearrange("(a p) d -> p a d", p=P)).then_inc(ld["wkq"], 16)
            sp.dma_start(wq[:], Wq.rearrange("(a p) d -> p a d", p=P)).then_inc(ld["wkq"], 16)
            sp.dma_start(ctx_nat[:, 0:h, :], full[:, 0:h, :]).then_inc(ld["ctx0"], 16)
            sp.dma_start(ctx_nat[:, h:FULL, :], full[:, h:FULL, :]).then_inc(ld["ctx1"], 16)
            sp.dma_start(ctx_nat[0:REST, FULL, :], ctx_1024[0, FULL * P:KEYS, :]).then_inc(ld["ctx2"], 16)
            sp.dma_start(wo[:], Wo.rearrange("(a p) d -> p a d", p=P)).then_inc(ld["wo"], 16)
            sp.dma_start(wv[:], Wv.rearrange("(a p) d -> p a d", p=P)).then_inc(ld["wv"], 16)
            for h in range(2):
                n = TILES // 2 * D
                sp.dma_start(X[:, h * n:(h + 1) * n], x_rows[:, h * n:(h + 1) * n]).then_inc(ld[f"x{h}"], 16)
            sp.dma_start(w1[:], W1.rearrange("e r d -> (e r) d").rearrange("(a p) d -> p a d", p=P)
                         ).then_inc(ld["w1"], 16)
            for dc in range(DC):
                sp.dma_start(w2[:, dc, :, :], W2[:, dc * P:(dc + 1) * P, :].rearrange("e p r -> p e r")
                             ).then_inc(ld["w2"], 16)
            for t in range(0, TILES, 2):
                sp.wait_ge(s_final, t + 2)
                sp.dma_start(out_rows[:, t * D:(t + 2) * D], X[:, t * D:(t + 2) * D]).then_inc(s_out, 16)
            sp.wait_ge(s_out, 16 * (TILES // 2))

        @block.gpsimd
        def _(pool):
            pool.memset(ident[:], 0.0).then_inc(s_ident0, 1)
            pool.wait_ge(s_ident0, 1)
            pool.affine_select(out=ident[:], in_=ident[:], compare_op=ALU.not_equal, fill=1.0, base=0,
                               pattern=[[-1, P]], channel_multiplier=1).then_inc(s_ident, 1)
            with nc.allow_non_contiguous_dma(reason="short vectors"):
                for dst, src in ((bq_col, bq), (bk_col, bk)):
                    pool.dma_start(dst[:], src.rearrange("(a p) -> p a", p=P)).then_inc(ld["bkq"], 16)
                pool.dma_start(bv_col[:], bv.rearrange("(a p) -> p a", p=P)).then_inc(ld["bvo"], 16)
                pool.dma_start(bo_row[:], bo.rearrange("(a d) -> a d", a=1)).then_inc(ld["bvo"], 16)
                for n, g in enumerate((g_xattn, g_ffn)):
                    pool.dma_start(gates[:, n:n + 1], g.rearrange("(a d) -> a d", a=1).to_broadcast([P, 1])
                                   ).then_inc(ld["gates"], 16)
                pool.dma_start(wg[:], Wg).then_inc(ld["wg"], 16)
                pool.dma_start(bg_wide[:], bg.rearrange("(a d) -> a d", a=1).to_broadcast([P, E])
                               ).then_inc(ld["wg"], 16)
            pool.memset(minus_half[:], -0.5).then_inc(s_const, 1)
            for e in range(E):
                pool.memset(expert_no[:, e:e + 1], float(e)).then_inc(s_const, 1)
            pool.memset(half_signs[:, 0:1], 0.5).then_inc(s_const, 1)
            pool.memset(half_signs[:, 1:2], -0.5).then_inc(s_const, 1)
            pool.memset(halves[:], 0.5).then_inc(s_const, 1)
            pool.memset(ones_row[:], 1.0).then_inc(s_const, 1)
            pool.wait_ge(s_const, E + 5)

            def x_moments(t, par):
                now, before = count(pool, t + 1), count(pool, t - 1)
                pool.wait_ge(s_const, E + 5)
                pool.wait_ge(s_xmv, now)
                if not isinstance(t, int) or t >= 2:
                    pool.wait_ge(s_xn, before)
                pool.tensor_scalar(x_ve[:, par:par + 1], x_mv[:, par, 1:2], EPS, None, ALU.add).then_inc(s_xve, 1)
                pool.wait_ge(s_xve, t + 1)
                pool.tensor_tensor(x_rstd[:, par:par + 1], x_ve[:, par:par + 1], minus_half[:, 0:1],
                                   ALU.pow).then_inc(s_xpow, 1)
                pool.wait_ge(s_const, E + 5)
                pool.wait_ge(s_xpow, now)
                pool.tensor_scalar(x_shift[:, par:par + 1], x_mv[:, par, 0:1], x_rstd[:, par:par + 1], -1.0,
                                   ALU.mult, ALU.mult).then_inc(s_xsh, 1)

            def vo_low(n):
                k = key_rows(n)
                pool.wait_ge(s_vo_hi, n + 1)
                pool.tensor_tensor(VO_lo[0:k, n, :], VO_sum[0:k, n % 2, :], f32(VO_hi[0:k, n, :]),
                                   ALU.subtract).then_inc(s_vo_lo, 1)

            for t in range(2):
                x_moments(t, t % 2)
            for n in range(KT):
                vo_low(n)
            x_moments(2, 0)

            def keep_z(t, par):
                pool.wait_ge(s_const, E + 5)
                pool.wait_ge(s_zmv, t + 1)
                pool.tensor_copy(z_all[:, bass.ds(t * 2, 2)], z_mv[:, par, :]).then_inc(s_zall, 1)

            x_moments(3, 1)
            with pool.Fori(0, TILES - 5, 2) as t:
                keep_z(t, 0)
                x_moments(t + 4, 0)
                keep_z(t + 1, 1)
                x_moments(t + 5, 1)
            for t in range(TILES - 4, TILES):
                keep_z(t, t % 2)

            mean = z_all[:].rearrange("p (t k) -> p t k", k=2)[:, :, 0]
            var = z_all[:].rearrange("p (t k) -> p t k", k=2)[:, :, 1]
            pool.wait_ge(s_zall, TILES)
            pool.tensor_scalar(z_ve[:], var, EPS, None, ALU.add).then_inc(s_zve, 1)
            pool.wait_ge(s_zve, 1)
            pool.tensor_tensor(z_rstd[:], z_ve[:], minus_half[:], ALU.pow).then_inc(s_zpow, 1)
            pool.tensor_scalar(z_negm[:], mean, -1.0, None, ALU.mult).then_inc(s_zneg, 1)
            pool.wait_ge(s_zneg, 1)
            pool.wait_ge(s_zpow, 1)
            pool.tensor_tensor(z_shift[:], z_negm[:], z_rstd[:], ALU.mult).then_inc(s_zsh, 1)

            def gate_hidden(t, par):
                pool.wait_ge(s_gelu, t + 1)
                pool.wait_ge(s_eg, t + 1)
                pool.tensor_tensor(hid[:, par], hid[:, par],
                                   expert_gate[:, par, :].unsqueeze(2).to_broadcast([P, E, R]),
                                   ALU.mult).then_inc(s_gated, 1)

            with pool.Fori(0, TILES - 1, 2) as t:
                gate_hidden(t, 0)
                gate_hidden(t + 1, 1)

        @block.tensor
        def _(pe):
            def three(dst, lhs_hi, lhs_lo, rhs_hi, rhs_lo, first, last):
                pe.matmul(dst, lhs_hi, rhs_hi, start=first, stop=False)
                pe.matmul(dst, lhs_hi, rhs_lo, start=False, stop=False)
                return pe.matmul(dst, lhs_lo, rhs_hi, start=False, stop=last)

            pe.wait_ge(ld["wkq"], 32)
            for jc in range(DC):
                for cc in range(DC):
                    mm = pe.matmul(T[jc][:, 0:D], wk[:, cc, jc * P:(jc + 1) * P], wq[:, cc, :],
                                   start=(cc == 0), stop=(cc == DC - 1))
                mm.then_inc(s_wkq_mm, 1)
            pe.wait_ge(s_ident, 1)
            for g in range(7):
                pe.wait_ge(ld["ctx0"] if g < 3 else ld["ctx1"] if g < 6 else ld["ctx2"], 16)
                if g >= 4:
                    pe.wait_ge(s_cT_lo, g - 3)
                tiles = [n for n in (2 * g, 2 * g + 1) if n < KT]
                for jc in range(DC):
                    for n in tiles:
                        k = key_rows(n)
                        at = jc * 2 * P + (n - 2 * g) * P
                        mm = pe.transpose(S[g % 4][:, at:at + k], ctx_nat[0:k, n, jc * P:(jc + 1) * P],
                                          ident[0:k, 0:k])
                mm.then_inc(s_cT, 1)
            pe.wait_ge(ld["bkq"], 32)
            pe.wait_ge(s_wide, 1)
            for i in range(2 * DC + 1):
                w, v = ((wq, bk_col), (wk, bq_col), (bq_wide, bk_col))[i // DC]
                jc = i % DC if i < 2 * DC else 0
                for cc in range(DC):
                    mm = pe.matmul(A[:, i:i + 1], w[:, cc, jc * P:(jc + 1) * P], v[:, cc:cc + 1],
                                   start=(cc == 0), stop=(cc == DC - 1))
            mm.then_inc(s_small_mm, 1)
            pe.wait_ge(ld["wo"], 16)
            pe.wait_ge(s_wkq_lo, 2)
            for cc in range(DC):
                for oc in range(DC):
                    mm = pe.transpose(T[0][:, cc * D + oc * P:cc * D + (oc + 1) * P],
                                      wo[:, oc, cc * P:(cc + 1) * P], ident[:])
            mm.then_inc(s_woT_mm, 1)
            pe.wait_ge(s_wkq_hi, 2)
            pe.wait_ge(s_cT_hi, 7)
            pe.wait_ge(s_cT_lo, 7)
            pe.wait_ge(s_pad, 2)
            for u in range(DC * 4):
                fc, (k0, kn) = u // 4, CHUNKS[u % 4]
                if u >= 4:
                    pe.wait_ge(s_kq_lo, u - 3)
                for jc in range(DC):
                    mm = three(S[u % 4][:, 0:kn], wkq_hi[:, jc, fc * P:(fc + 1) * P],
                               wkq_lo[:, jc, fc * P:(fc + 1) * P], ctxT_hi[:, jc, k0:k0 + kn],
                               ctxT_lo[:, jc, k0:k0 + kn], jc == 0, jc == DC - 1)
                mm.then_inc(s_kq_mm, 1)
            pe.wait_ge(s_woT, 1)
            pe.wait_ge(ld["wv"], 16)
            for jc in range(DC):
                for cc in range(DC):
                    mm = pe.matmul(T[1][:, jc * D:(jc + 1) * D], wv[:, cc, jc * P:(jc + 1) * P], woT[:, cc, :],
                                   start=(cc == 0), stop=(cc == DC - 1))
            mm.then_inc(s_wvo_mm, 1)
            pe.wait_ge(ld["bvo"], 32)
            pe.wait_ge(s_wide, 2)
            pe.wait_ge(s_const, E + 5)
            pe.wait_ge(s_small, 1)
            for cc in range(DC):
                pe.matmul(A[:, 0:D], bv_wide[:, cc, :], woT[:, cc, :], start=(cc == 0), stop=False)
            pe.matmul(A[:, 0:D], ones_row[:], bo_row[:], start=False, stop=True).then_inc(s_vb_mm, 1)
            pe.wait_ge(s_bqwk, 1)
            for c, (k0, kn) in enumerate(CHUNKS):
                pe.wait_ge(s_kq_lo, 5 + c)
                for jc in range(DC):
                    mm = three(S[c][:, 0:kn], bqwk_hi[:, jc, :], bqwk_lo[:, jc, :], ctxT_hi[:, jc, k0:k0 + kn],
                               ctxT_lo[:, jc, k0:k0 + kn], jc == 0, jc == DC - 1)
                mm.then_inc(s_kb_mm, 1)

            def transpose_xn(t, par):
                pe.wait_ge(s_xn, t + 1)
                if not isinstance(t, int) or t >= 1:
                    pe.wait_ge(s_xnT_lo, t)
                for dc in range(DC):
                    mm = pe.transpose(B[:, dc * P:(dc + 1) * P], xn[:, par, dc * P:(dc + 1) * P], ident[:])
                mm.then_inc(s_xnT, 1)

            transpose_xn(0, 0)
            pe.wait_ge(s_wvo_hi, 1)
            pe.wait_ge(s_wvo_lo, 1)
            pe.wait_ge(s_woT_lo, 1)
            for n in range(KT):
                k = key_rows(n)
                if n >= 2:
                    pe.wait_ge(s_vo_sum, n - 1)
                for jc in range(DC):
                    mm = three(T[n % 2][0:k, 0:D], ctxT_hi[:, jc, n * P:n * P + k], ctxT_lo[:, jc, n * P:n * P + k],
                               wvo_hi[:, jc, :], wvo_lo[:, jc, :], jc == 0, jc == DC - 1)
                mm.then_inc(s_vo_mm, 1)
            transpose_xn(1, 1)

            def scores(t, par, first=False):
                pe.wait_ge(s_xnT_hi, t + 1)
                pe.wait_ge(s_xnT_lo, t + 1)
                for c, (k0, kn) in enumerate(CHUNKS):
                    if first:
                        pe.wait_ge(s_kb, c + 1)
                    else:
                        pe.wait_ge(s_biased, t * 4 + (c - 3))
                    for dc in range(DC):
                        mm = three(S[c][:, 0:kn], xnT_hi[:, par, dc, :], xnT_lo[:, par, dc, :],
                                   KQ_hi[:, dc, k0:k0 + kn], KQ_lo[:, dc, k0:k0 + kn], dc == 0, dc == DC - 1)
                    mm.then_inc(s_score, 1)

            def attend(t, par, first=False):
                if first:
                    pe.wait_ge(s_vb, 1)
                else:
                    pe.wait_ge(s_x1, t)
                for dc in range(DC):
                    three(A[:, D:2 * D], xnT_hi[:, par, dc, :], xnT_lo[:, par, dc, :],
                          woT_hi[:, dc, :], woT_lo[:, dc, :], dc == 0, dc == DC - 1)

                def turn(g):
                    pe.wait_ge(s_exp, t * 2 + (1 if g == 0 else 2))
                    if not (first and g < 2):
                        pe.wait_ge(s_pT_lo, t * 4 + (g - 1))
                    for n in GROUPS[g]:
                        k, at = key_rows(n), (n % 4) * P
                        mm = pe.transpose(T[g % 2][0:k, at:at + P], probs[:, par, n * P:n * P + k], ident[:])
                    mm.then_inc(s_pT, 1)

                def weigh(g):
                    pe.wait_ge(s_pT_hi, t * 4 + (g + 1))
                    pe.wait_ge(s_pT_lo, t * 4 + (g + 1))
                    for n in GROUPS[g]:
                        k = key_rows(n)
                        mm = three(A[:, 0:D], pT_hi[0:k, n, :], pT_lo[0:k, n, :], VO_hi[0:k, n, :],
                                   VO_lo[0:k, n, :], n == 0, n == KT - 1)
                    if g == 3:
                        mm.then_inc(s_attn, 1)

                turn(0)
                turn(1)
                weigh(0)
                turn(2)
                weigh(1)
                turn(3)
                weigh(2)
                weigh(3)

            pe.wait_ge(s_kq_hi, 8)
            scores(0, 0, first=True)
            pe.wait_ge(s_vo_lo, KT)
            pe.wait_ge(s_vo_sum, KT)
            for t in range(2):
                scores(t + 1, (t + 1) % 2)
                if t == 0:
                    pe.wait_ge(s_woT_hi, 1)
                attend(t, t % 2, first=(t == 0))
                transpose_xn(t + 2, t % 2)
            with pe.Fori(2, TILES - 3, 2) as t:
                for h in range(2):
                    scores(t + (h + 1), (h + 1) % 2)
                    attend(t + h, h)
                    transpose_xn(t + (h + 2), h)
            scores(TILES - 1, 1)
            attend(TILES - 2, 0)
            attend(TILES - 1, 1)

            pe.wait_ge(ld["w1"], 16)
            for dc in range(DC):
                pe.wait_ge(s_biased, 4 * TILES)
                for et in range(ET):
                    mm = pe.transpose(S[dc][:, et * P:(et + 1) * P], w1[:, et, dc * P:(dc + 1) * P], ident[:])
                mm.then_inc(s_w1T_mm, 1)
            pe.wait_ge(ld["wg"], 32)
            pe.wait_ge(s_xnT_lo, TILES)
            for dc in range(DC):
                mm = pe.transpose(B[:, dc * E:(dc + 1) * E], wg[:, dc * P:(dc + 1) * P], ident[0:E, 0:E])
            mm.then_inc(s_wgT_mm, 1)
            pe.wait_ge(ld["w2"], 16 * DC)
            for b in range(2):
                for et in (2 * b, 2 * b + 1):
                    for dc in range(DC):
                        at = (et % 2) * D + dc * P
                        mm = pe.transpose(S[2 + b][:, at:at + P],
                                          w2[:, dc].rearrange("p e r -> p (e r)")[:, et * P:(et + 1) * P], ident[:])
                mm.then_inc(s_w2T_mm, 1)

            def transpose_z(t, par, first=False):
                pe.wait_ge(s_z, t + 1)
                pe.wait_ge(s_wgT_lo, 1) if first else pe.wait_ge(s_zT_lo, t)
                for dc in range(DC):
                    mm = pe.transpose(B[:, dc * P:(dc + 1) * P], zb[:, par, dc * P:(dc + 1) * P], ident[:])
                mm.then_inc(s_zT, 1)

            def up(t, par, first=False):
                pe.wait_ge(s_zT_hi, t + 1)
                pe.wait_ge(s_zT_lo, t + 1)
                if not first:
                    pe.wait_ge(s_gelu, t - 1)
                for b in range(2):
                    for dc in range(DC):
                        mm = three(S[2 * par + b][:, 0:UPW], zT_hi[:, par, dc, :], zT_lo[:, par, dc, :],
                                   w1T_hi[:, dc, b, :], w1T_lo[:, dc, b, :], dc == 0, dc == DC - 1)
                mm.then_inc(s_up, 1)

            def transpose_hidden(t, par, first=False):
                pe.wait_ge(s_gated, t + 1)
                if not first:
                    pe.wait_ge(s_hT_lo, t - 1)
                flat = hid[:, par].rearrange("p e r -> p (e r)")
                for et in range(ET):
                    mm = pe.transpose(T[par][:, et * P:(et + 1) * P], flat[:, et * P:(et + 1) * P], ident[:])
                mm.then_inc(s_hT, 1)

            def down(t, par, first=False):
                pe.wait_ge(s_hT_hi, t + 1)
                pe.wait_ge(s_hT_lo, t + 1)
                pe.wait_ge(s_x1, TILES) if first else pe.wait_ge(s_final, t)
                for et in range(ET):
                    mm = three(A[:, 0:D], hT_hi[:, par, et, :], hT_lo[:, par, et, :],
                               w2T_hi[:, et, :], w2T_lo[:, et, :], et == 0, et == ET - 1)
                mm.then_inc(s_down, 1)

            transpose_z(0, 0, first=True)
            pe.wait_ge(s_w1T_hi, 2)
            pe.wait_ge(s_w1T_lo, 2)
            pe.wait_ge(s_wgT_hi, 1)
            up(0, 0, first=True)
            transpose_z(1, 1)
            pe.wait_ge(s_w2T_hi, 2)
            pe.wait_ge(s_w2T_lo, 2)
            up(1, 1, first=True)
            transpose_z(2, 0)
            transpose_hidden(0, 0, first=True)
            up(2, 0)
            transpose_z(3, 1)
            down(0, 0, first=True)
            transpose_hidden(1, 1, first=True)
            up(3, 1)
            transpose_z(4, 0)
            down(1, 1)
            transpose_hidden(2, 0)
            with pe.Fori(4, TILES - 3, 2) as u:
                for h in range(2):
                    up(u + h, h)
                    transpose_z(u + (h + 1), 1 - h)
                    down(u + (h - 2), h)
                    transpose_hidden(u + (h - 1), 1 - h)
            up(TILES - 2, 0)
            transpose_z(TILES - 1, 1)
            down(TILES - 4, 0)
            transpose_hidden(TILES - 3, 1)
            up(TILES - 1, 1)
            down(TILES - 3, 1)
            transpose_hidden(TILES - 2, 0)
            down(TILES - 2, 0)
            transpose_hidden(TILES - 1, 1)
            down(TILES - 1, 1)

        @block.scalar
        def _(act):
            act.preload_act_table(ACT.Exp)
            for jc in range(DC):
                act.wait_ge(s_wkq_mm, jc + 1)
                act.activation(wkq_hi[:, jc, :], T[jc][:, 0:D], ACT.Copy).then_inc(s_wkq_hi, 1)
            for g in range(7):
                act.wait_ge(s_cT, g + 1)
                act.activation(*ctxT_part(ctxT_hi, g), ACT.Copy).then_inc(s_cT_hi, 1)
            act.wait_ge(s_woT_mm, 1)
            flat = lambda w: w[:].rearrange("p a d -> p (a d)")
            act.activation(flat(woT), T[0][:], ACT.Copy).then_inc(s_woT, 1)
            act.activation(flat(woT_hi), T[0][:], ACT.Copy).then_inc(s_woT_hi, 1)
            act.wait_ge(s_small, 1)
            for u in range(DC * 4):
                fc, (k0, kn) = u // 4, CHUNKS[u % 4]
                act.wait_ge(s_kq_mm, u + 1)
                act.activation(KQ_hi[:, fc, k0:k0 + kn], S[u % 4][:, 0:kn], ACT.Identity,
                               bias=small[:, fc:fc + 1]).then_inc(s_kq_hi, 1)
            act.wait_ge(s_wvo_mm, 1)
            act.activation(flat(wvo_hi), T[1][:], ACT.Copy).then_inc(s_wvo_hi, 1)
            act.wait_ge(s_vb_mm, 1)
            act.activation(vo_bias[:], A[:, 0:D], ACT.Copy).then_inc(s_vb, 1)
            act.wait_ge(ld["gates"], 32)
            act.activation(gate_tanh[:], gates[:], ACT.Tanh).then_inc(s_gate, 1)
            act.wait_ge(ld["x0"], 16)

            def normalize_x(t, par):
                act.wait_ge(s_xsh, t + 1)
                if not isinstance(t, int) or t >= 2:
                    act.wait_ge(s_xnT, t - 1)
                act.activation(xn[:, par, :], tile_of(t), ACT.Identity, bias=x_shift[:, par:par + 1],
                               scale=x_rstd[:, par:par + 1]).then_inc(s_xn, 1)

            def xnT_high(t, par):
                act.wait_ge(s_xnT, t + 1)
                act.activation(xnT_hi[:, par].rearrange("p a d -> p (a d)"), B[:, 0:D], ACT.Copy
                               ).then_inc(s_xnT_hi, 1)

            def exponentials(t, par, h):
                if h == 0:
                    act.wait_ge(s_ebias, t + 1)
                    if not isinstance(t, int) or t >= 2:
                        act.wait_ge(s_sum, t - 1)
                cut = slice(0, HALF) if h == 0 else slice(HALF, KEYS)
                act.activation(probs[:, par, cut], probs[:, par, cut], ACT.Exp, bias=exp_bias[:, par:par + 1],
                               scale=SCALE, accum_out=half_sum[:, par, h:h + 1]).then_inc(s_exp, 1)

            def pT_high(t, g):
                act.wait_ge(s_pT, t * 4 + (g + 1))
                rows, dst, src = pT_part(pT_hi, g)
                act.activation(dst, src, ACT.Copy).then_inc(s_pT_hi, 1)

            normalize_x(0, 0)
            normalize_x(1, 1)
            xnT_high(0, 0)
            for n in range(KT):
                k = key_rows(n)
                act.wait_ge(s_vo_sum, n + 1)
                act.activation(VO_hi[0:k, n, :], VO_sum[0:k, n % 2, :], ACT.Copy).then_inc(s_vo_hi, 1)
            xnT_high(1, 1)
            exponentials(0, 0, 0)
            exponentials(0, 0, 1)

            def step(t, par, ahead, two_ahead):
                if two_ahead:
                    normalize_x(t + 2, par)
                pT_high(t, 0)
                pT_high(t, 1)
                if ahead:
                    exponentials(t + 1, 1 - par, 0)
                pT_high(t, 2)
                if ahead:
                    exponentials(t + 1, 1 - par, 1)
                pT_high(t, 3)
                if two_ahead:
                    xnT_high(t + 2, par)

            act.wait_ge(ld["x1"], 16)
            step(0, 0, True, True)
            step(1, 1, True, True)
            with act.Fori(2, TILES - 3, 2) as t:
                step(t, 0, True, True)
                step(t + 1, 1, True, True)
            step(TILES - 2, 0, True, False)
            step(TILES - 1, 1, False, False)

            act.preload_act_table(ACT.Gelu)
            for dc in range(DC):
                act.wait_ge(s_w1T_mm, dc + 1)
                act.activation(w1T_hi[:, dc, :, 0:ER // 2], S[dc][:].rearrange("p (b n) -> p b n", b=2), ACT.Copy
                               ).then_inc(s_w1T_hi, 1)
            act.wait_ge(s_wgT_mm, 1)
            act.activation(w1T_hi[:, :, :, ER // 2:UPW], wgT_part(), ACT.Copy).then_inc(s_wgT_hi, 1)

            def normalize_z(t, par):
                if not isinstance(t, int) or t >= 2:
                    act.wait_ge(s_zT, t - 1)
                act.activation(zb[:, par, :], tile_of(t), ACT.Identity, bias=z_shift[:, bass.ds(t, 1)],
                               scale=z_rstd[:, bass.ds(t, 1)]).then_inc(s_z, 1)

            def zT_high(t, par):
                act.wait_ge(s_zT, t + 1)
                act.activation(zT_hi[:, par].rearrange("p a d -> p (a d)"), B[:, 0:D], ACT.Copy
                               ).then_inc(s_zT_hi, 1)

            def gelu(t, par):
                act.wait_ge(s_logit, t + 1)
                if not isinstance(t, int) or t >= 2:
                    act.wait_ge(s_hT, t - 1)
                for b in range(2):
                    ins = act.activation(hid[:, par].rearrange("p (b e) r -> p b (e r)", b=2)[:, b, :],
                                         S[2 * par + b][:, 0:ER // 2], ACT.Gelu)
                    if b == 1:
                        ins.then_inc(s_gelu, 1)

            def gate_of_two(t, par):
                act.wait_ge(s_diff, t + 1)
                act.activation(top_tanh[:, par:par + 1], top_diff[:, par:par + 1], ACT.Tanh, scale=0.5
                               ).then_inc(s_ttanh, 1)

            def hT_high(t, par):
                act.wait_ge(s_hT, t + 1)
                act.activation(hT_hi[:, par].rearrange("p a d -> p (a d)"), T[par][:], ACT.Copy
                               ).then_inc(s_hT_hi, 1)

            act.wait_ge(s_zsh, 1)
            normalize_z(0, 0)
            normalize_z(1, 1)
            for b in range(2):
                act.wait_ge(s_w2T_mm, b + 1)
                act.activation(w2T_hi[:, 2 * b:2 * b + 2, :].rearrange("p a d -> p (a d)"), S[2 + b][:], ACT.Copy
                               ).then_inc(s_w2T_hi, 1)
            zT_high(0, 0)

            def step2(u, par, z1=True, hidden=True, z2=True):
                if z1:
                    zT_high(u + 1, 1 - par)
                gelu(u, par)
                gate_of_two(u, par)
                if hidden:
                    hT_high(u - 1, 1 - par)
                if z2:
                    normalize_z(u + 2, par)

            step2(0, 0, hidden=False)
            step2(1, 1)
            step2(2, 0)
            step2(3, 1)
            with act.Fori(4, TILES - 3, 2) as u:
                step2(u, 0)
                step2(u + 1, 1)
            step2(TILES - 2, 0, z2=False)
            step2(TILES - 1, 1, z1=False, z2=False)
            hT_high(TILES - 1, 1)

        @block.vector
        def _(dve):
            dve.memset(f32(ctxT_hi[:, :, KEYS:KPAD]), 0.0).then_inc(s_pad, 1)
            dve.memset(f32(ctxT_lo[:, :, KEYS:KPAD]), 0.0).then_inc(s_pad, 1)
            dve.wait_ge(ld["bkq"], 32)
            dve.tensor_copy(bq_wide[:], bq_col[:].unsqueeze(2).to_broadcast([P, DC, P])).then_inc(s_wide, 1)
            dve.wait_ge(ld["bvo"], 32)
            dve.tensor_copy(bv_wide[:], bv_col[:].unsqueeze(2).to_broadcast([P, DC, P])).then_inc(s_wide, 1)
            for jc in range(DC):
                dve.wait_ge(s_wkq_hi, jc + 1)
                dve.tensor_tensor(wkq_lo[:, jc, :], T[jc][:, 0:D], f32(wkq_hi[:, jc, :]), ALU.subtract
                                  ).then_inc(s_wkq_lo, 1)

            def ctx_low(g):
                dve.wait_ge(s_cT_hi, g + 1)
                dst, src = ctxT_part(ctxT_lo, g)
                dve.tensor_tensor(dst, src, f32(ctxT_part(ctxT_hi, g)[0]), ALU.subtract).then_inc(s_cT_lo, 1)

            for g in range(7):
                ctx_low(g)
            dve.wait_ge(s_small_mm, 1)
            dve.tensor_copy(small[:, 0:5], A[:, 0:5]).then_inc(s_small, 1)
            dve.wait_ge(s_small, 1)
            wide = small[:, 2:4].unsqueeze(2).to_broadcast([P, DC, P])
            dve.tensor_copy(bqwk_hi[:], wide).then_inc(s_bqwk_hi, 1)
            dve.wait_ge(s_bqwk_hi, 1)
            dve.tensor_tensor(bqwk_lo[:], wide, f32(bqwk_hi[:]), ALU.subtract).then_inc(s_bqwk, 1)
            dve.wait_ge(s_woT_hi, 1)
            flat = lambda w: w[:].rearrange("p a d -> p (a d)")
            dve.tensor_tensor(flat(woT_lo), T[0][:], f32(flat(woT_hi)), ALU.subtract).then_inc(s_woT_lo, 1)
            for u in range(DC * 4):
                fc, (k0, kn) = u // 4, CHUNKS[u % 4]
                dve.wait_ge(s_kq_hi, u + 1)
                dve.scalar_tensor_tensor(out=KQ_lo[:, fc, k0:k0 + kn], in0=S[u % 4][:, 0:kn],
                                         scalar=small[:, fc:fc + 1], in1=f32(KQ_hi[:, fc, k0:k0 + kn]),
                                         op0=ALU.add, op1=ALU.subtract).then_inc(s_kq_lo, 1)
            dve.wait_ge(s_wvo_hi, 1)
            dve.tensor_tensor(flat(wvo_lo), T[1][:], f32(flat(wvo_hi)), ALU.subtract).then_inc(s_wvo_lo, 1)

            def x_statistics(t, par):
                now, before = count(dve, t + 1), count(dve, t - 1)
                dve.wait_ge(ld["x0"], 16)
                if not isinstance(t, int) or t >= 2:
                    dve.wait_ge(s_xsh, before)
                dve.bn_stats(x_bn[:, par, :], tile_of(t)).then_inc(s_xbn, 1)
                dve.wait_ge(ld["x0"], 16)
                dve.wait_ge(s_xbn, now)
                dve.bn_aggr(x_mv[:, par, :], x_bn[:, par, :]).then_inc(s_xmv, 1)

            dve.wait_ge(ld["x0"], 16)
            x_statistics(0, 0)
            x_statistics(1, 1)
            for c, (k0, kn) in enumerate(CHUNKS):
                dve.wait_ge(s_kb_mm, c + 1)
                dve.tensor_scalar(key_bias[:, k0:k0 + kn], S[c][:, 0:kn], small[:, 4:5], None, ALU.add
                                  ).then_inc(s_kb, 1)
            dve.wait_ge(s_kb, 4)

            def xnT_low(t, par):
                dve.wait_ge(s_xnT_hi, t + 1)
                dst, hi = (w[:, par].rearrange("p a d -> p (a d)") for w in (xnT_lo, xnT_hi))
                dve.tensor_tensor(dst, B[:, 0:D], f32(hi), ALU.subtract).then_inc(s_xnT_lo, 1)

            xnT_low(0, 0)
            dve.wait_ge(s_vb, 1)
            for n in range(KT):
                k = key_rows(n)
                dve.wait_ge(s_vo_mm, n + 1)
                if n >= 2:
                    dve.wait_ge(s_vo_lo, n - 1)
                dve.tensor_tensor(VO_sum[0:k, n % 2, :], T[n % 2][0:k, 0:D], vo_bias[0:k, :], ALU.add
                                  ).then_inc(s_vo_sum, 1)
            xnT_low(1, 1)

            def scores_and_max(t, par):
                if not isinstance(t, int) or t >= 2:
                    dve.wait_ge(s_pT, t * 4 - 4)
                for c, (k0, kn) in enumerate(CHUNKS):
                    n = min(kn, KEYS - k0)
                    now = count(dve, t * 4 + (c + 1))
                    dve.wait_ge(s_kb, 4)
                    dve.wait_ge(s_score, now)
                    dve.tensor_tensor_reduce(
                        out=probs[:, par, k0:k0 + n], in0=S[c][:, 0:n], in1=key_bias[:, k0:k0 + n], scale=1.0,
                        scalar=-3.0e38, op0=ALU.add, op1=ALU.max, accum_out=chunk_max[:, par, c:c + 1]
                    ).then_inc(s_biased, 1)
                dve.wait_ge(s_biased, t * 4 + 4)
                dve.reduce_max(row_max[:, par:par + 1], chunk_max[:, par, :], AX_X).then_inc(s_max, 1)
                dve.wait_ge(s_max, t + 1)
                dve.tensor_scalar(exp_bias[:, par:par + 1], row_max[:, par:par + 1], -SCALE, None, ALU.mult
                                  ).then_inc(s_ebias, 1)

            def pT_low(t, g):
                dve.wait_ge(s_pT_hi, t * 4 + (g + 1))
                rows, dst, src = pT_part(pT_lo, g)
                dve.tensor_tensor(dst, src, f32(pT_part(pT_hi, g)[1]), ALU.subtract).then_inc(s_pT_lo, 1)

            def row_gains(t, par):
                dve.wait_ge(s_exp, t * 2 + 2)
                if not isinstance(t, int) or t >= 1:
                    dve.wait_ge(s_inv, t)
                dve.tensor_tensor(row_sum[:], half_sum[:, par, 0:1], half_sum[:, par, 1:2], ALU.add
                                  ).then_inc(s_sum, 1)
                dve.wait_ge(s_sum, t + 1)
                if not isinstance(t, int) or t >= 1:
                    dve.wait_ge(s_gain, t)
                dve.reciprocal(row_inv[:], row_sum[:]).then_inc(s_inv, 1)
                dve.wait_ge(s_inv, t + 1)
                if not isinstance(t, int) or t >= 1:
                    dve.wait_ge(s_x1, t)
                dve.tensor_scalar(row_gain[:], row_inv[:], gate_tanh[:, 0:1], None, ALU.mult).then_inc(s_gain, 1)

            def attention_out(t, par):
                dve.wait_ge(s_attn, t + 1)
                dve.scalar_tensor_tensor(out=resid[:], in0=A[:, D:2 * D], scalar=gate_tanh[:, 0:1], in1=tile_of(t),
                                         op0=ALU.mult, op1=ALU.add).then_inc(s_resid, 1)
                dve.wait_ge(s_resid, t + 1)
                dve.wait_ge(s_gain, t + 1)
                dve.scalar_tensor_tensor(out=tile_of(t), in0=A[:, 0:D], scalar=row_gain[:], in1=resid[:],
                                         op0=ALU.mult, op1=ALU.add).then_inc(s_x1, 1)
                dve.wait_ge(ld["x1"], 16)
                dve.wait_ge(s_x1, t + 1)
                if not isinstance(t, int) or t >= 1:
                    dve.wait_ge(s_zmv, t)
                dve.bn_stats(z_bn[:], tile_of(t)).then_inc(s_zbn, 1)
                now, before = count(dve, t + 1), count(dve, t - 1)
                dve.wait_ge(ld["x1"], 16)
                dve.wait_ge(s_zbn, now)
                if not isinstance(t, int) or t >= 2:
                    dve.wait_ge(s_zall, before)
                dve.bn_aggr(z_mv[:, par, :], z_bn[:]).then_inc(s_zmv, 1)

            dve.wait_ge(s_gate, 1)
            dve.tensor_scalar(ffn_scale[:], gate_tanh[:, 1:2], LORA_SCALING, None, ALU.mult).then_inc(s_fscale, 1)
            x_statistics(2, 0)
            scores_and_max(0, 0)
            dve.wait_ge(ld["x1"], 16)

            def step(t, par, out_before=True, ahead=True, two_ahead=True, three_ahead=True):
                if out_before:
                    attention_out(t - 1, 1 - par)
                if ahead:
                    scores_and_max(t + 1, 1 - par)
                pT_low(t, 0)
                pT_low(t, 1)
                row_gains(t, par)
                pT_low(t, 2)
                pT_low(t, 3)
                if three_ahead:
                    x_statistics(t + 3, 1 - par)
                if two_ahead:
                    xnT_low(t + 2, par)

            step(0, 0, out_before=False)
            step(1, 1)
            with dve.Fori(2, TILES - 5, 2) as t:
                step(t, 0)
                step(t + 1, 1)
            step(TILES - 4, 0)
            step(TILES - 3, 1, three_ahead=False)
            step(TILES - 2, 0, two_ahead=False, three_ahead=False)
            step(TILES - 1, 1, ahead=False, two_ahead=False, three_ahead=False)
            attention_out(TILES - 1, 1)

            for dc in range(DC):
                dve.wait_ge(s_w1T_hi, dc + 1)
                dve.tensor_tensor(w1T_lo[:, dc, :, 0:ER // 2], S[dc][:].rearrange("p (b n) -> p b n", b=2),
                                  f32(w1T_hi[:, dc, :, 0:ER // 2]), ALU.subtract).then_inc(s_w1T_lo, 1)
            dve.wait_ge(s_wgT_hi, 1)
            dve.tensor_tensor(w1T_lo[:, :, :, ER // 2:UPW], wgT_part(), f32(w1T_hi[:, :, :, ER // 2:UPW]),
                              ALU.subtract).then_inc(s_wgT_lo, 1)
            for b in range(2):
                dve.wait_ge(s_w2T_hi, b + 1)
                dst, hi = (w[:, 2 * b:2 * b + 2, :].rearrange("p a d -> p (a d)") for w in (w2T_lo, w2T_hi))
                dve.tensor_tensor(dst, S[2 + b][:], f32(hi), ALU.subtract).then_inc(s_w2T_lo, 1)

            def zT_low(t, par):
                dve.wait_ge(s_zT_hi, t + 1)
                dst, hi = (w[:, par].rearrange("p a d -> p (a d)") for w in (zT_lo, zT_hi))
                dve.tensor_tensor(dst, B[:, 0:D], f32(hi), ALU.subtract).then_inc(s_zT_lo, 1)

            def route(t, par):
                n = E // 2
                dve.wait_ge(s_up, t + 1)
                if not isinstance(t, int) or t >= 2:
                    dve.wait_ge(s_eg, t - 1)
                for b in range(2):
                    ins = dve.tensor_tensor(logits[:, par, b * n:(b + 1) * n], S[2 * par + b][:, ER // 2:UPW],
                                            bg_wide[:, b * n:(b + 1) * n], ALU.add)
                    ins.then_inc(s_logit2 if b == 0 else s_logit, 1)
                dve.wait_ge(ld["wg"], 32)
                dve.wait_ge(s_logit2, t + 1)
                dve.wait_ge(s_logit, t + 1)
                dve.max(top8[:, par, :], logits[:, par, :]).then_inc(s_top, 1)
                dve.wait_ge(ld["wg"], 32)
                dve.wait_ge(s_top, t + 1)
                dve.max_index(top_idx[:, par, :], top8[:, par, :], logits[:, par, :]).then_inc(s_idx, 1)
                dve.tensor_tensor(top_diff[:, par:par + 1], top8[:, par, 0:1], top8[:, par, 1:2], ALU.subtract
                                  ).then_inc(s_diff, 1)

            def spread_gates(t, par):
                dve.wait_ge(s_ttanh, t + 1)
                dve.scalar_tensor_tensor(out=top_gate[:, par, :], in0=half_signs[:], scalar=top_tanh[:, par:par + 1],
                                         in1=halves[:], op0=ALU.mult, op1=ALU.add).then_inc(s_tgate, 1)
                dve.wait_ge(s_idx, t + 1)
                dve.tensor_tensor(is_top[:, par], expert_no[:].unsqueeze(1).to_broadcast([P, 2, E]),
                                  top_idx[:, par, 0:2].unsqueeze(2).to_broadcast([P, 2, E]), ALU.is_equal
                                  ).then_inc(s_is, 1)
                dve.wait_ge(s_tgate, t + 1)
                dve.wait_ge(s_is, t + 1)
                dve.tensor_tensor(gate_two[:, par], is_top[:, par],
                                  top_gate[:, par, :].unsqueeze(2).to_broadcast([P, 2, E]), ALU.mult
                                  ).then_inc(s_two, 1)
                dve.wait_ge(s_two, t + 1)
                if not isinstance(t, int) or t >= 2:
                    dve.wait_ge(s_gated, t - 1)
                dve.tensor_tensor(expert_gate[:, par, :], gate_two[:, par, 0, :], gate_two[:, par, 1, :], ALU.add
                                  ).then_inc(s_eg, 1)

            def hT_low(t, par):
                dve.wait_ge(s_hT_hi, t + 1)
                dst, hi = (w[:, par].rearrange("p a d -> p (a d)") for w in (hT_lo, hT_hi))
                dve.tensor_tensor(dst, T[par][:], f32(hi), ALU.subtract).then_inc(s_hT_lo, 1)

            def finish(t):
                dve.wait_ge(s_down, t + 1)
                dve.scalar_tensor_tensor(out=tile_of(t), in0=A[:, 0:D], scalar=ffn_scale[:], in1=tile_of(t),
                                         op0=ALU.mult, op1=ALU.add).then_inc(s_final, 1)

            dve.wait_ge(s_const, E + 5)
            dve.wait_ge(s_fscale, 1)
            dve.wait_ge(ld["wg"], 32)
            zT_low(0, 0)

            def step2(u, par, z1=True, hidden=True, last=True):
                route(u, par)
                if z1:
                    zT_low(u + 1, 1 - par)
                spread_gates(u, par)
                if hidden:
                    hT_low(u - 1, 1 - par)
                if last:
                    finish(u - 2)

            step2(0, 0, hidden=False, last=False)
            step2(1, 1, last=False)
            step2(2, 0)
            step2(3, 1)
            with dve.Fori(4, TILES - 3, 2) as u:
                step2(u, 0)
                step2(u + 1, 1)
            step2(TILES - 2, 0)
            step2(TILES - 1, 1, z1=False)
            finish(TILES - 2)
            hT_low(TILES - 1, 1)
            finish(TILES - 1)


_INS = ["x", "ctx_1024", "g_xattn", "g_ffn", "L0_xattn_Wq", "L0_xattn_bq", "L0_xattn_Wk", "L0_xattn_bk",
        "L0_xattn_Wv", "L0_xattn_bv", "L0_xattn_Wo", "L0_xattn_bo", "L0_ffn_Wg", "L0_ffn_bg", "L0_ffn_W1",
        "L0_ffn_W2"]


def kernel(**inputs):
    import numpy as _np
    import concourse.bacc as _bacc
    from concourse import mybir as _mybir
    from concourse.bass_utils import run_bass_kernel_spmd as _run

    nc = _bacc.Bacc("TRN2", target_bir_lowering=False, num_devices=1)
    arrays, args = {}, []
    for name in _INS:
        a = _np.ascontiguousarray(inputs[name])
        arrays[f"in_{name}"] = a
        args.append(nc.dram_tensor(f"in_{name}", a.shape, _mybir.dt.from_np(a.dtype), kind="ExternalInput").ap())
    shape = tuple(inputs["x"].shape)
    args.append(nc.dram_tensor("out_0", shape, _mybir.dt.float32, kind="ExternalOutput").ap())
    flamingo_layer(nc, *args)
    r = _run(nc, [arrays], core_ids=[0])
    return r.results[0]["out_0"]
```

```python
from contextlib import ExitStack

import concourse.bass as bass
from concourse import mybir

ALU = mybir.AluOpType
ACT = mybir.ActivationFunctionType
AX_X = mybir.AxisListType.X
F32 = mybir.dt.float32
F32R = mybir.dt.float32r
U32 = mybir.dt.uint32

P = 128
EPS = 1e-5
LORA_SCALING = 2.0


def flamingo_layer(nc, x, ctx_1024, g_xattn, g_ffn, Wq, bq, Wk, bk, Wv, bv, Wo, bo, Wg, bg, W1, W2, out):
    SQ, D = x.shape[1], x.shape[2]
    KEYS = ctx_1024.shape[1]
    E, R, _ = W1.shape
    TILES = SQ // P
    DC = D // P
    FULL = KEYS // P
    REST = KEYS - FULL * P
    KT = FULL + 1
    KPAD = KEYS + KEYS % 2
    CH = 402
    CHUNKS = [(c * CH, min(CH, KPAD - c * CH)) for c in range(4)]
    GROUPS = [range(g * 4, min(g * 4 + 4, KT)) for g in range(4)]
    HALF = 2 * CH
    ER = E * R
    ET = ER // P
    UPW = ER // 2 + E // 2
    SCALE = float(D) ** -0.5
    assert D == 2 * P and REST > 0 and CHUNKS[-1][0] + CHUNKS[-1][1] == KPAD and ER == 512
    assert TILES % 2 == 0 and TILES >= 8

    with ExitStack() as ctx:
        def sb(name, shape, dt=F32):
            return ctx.enter_context(nc.sbuf_tensor(name, shape, dt))

        def bank(name):
            return ctx.enter_context(nc.psum_tensor(name, [P, 512], F32))

        def sem(name):
            return ctx.enter_context(nc.semaphore(name))

        X = sb("X", [P, TILES * D])
        ident = sb("ident", [P, P])
        ctx_nat = sb("ctx_nat", [P, KT, D])
        ctxT_hi = sb("ctxT_hi", [P, DC, KPAD], F32R)
        ctxT_lo = sb("ctxT_lo", [P, DC, KPAD], F32R)
        wq = sb("wq", [P, DC, D + 1])
        wk = sb("wk", [P, DC, D])
        wv = sb("wv", [P, DC, D])
        wo = sb("wo", [P, DC, D])
        woT = sb("woT", [P, DC, D])
        woT_hi = sb("woT_hi", [P, DC, D], F32R)
        woT_lo = sb("woT_lo", [P, DC, D], F32R)
        wkq_hi = sb("wkq_hi", [P, DC, D], F32R)
        wkq_lo = sb("wkq_lo", [P, DC, D], F32R)
        wvo_hi = sb("wvo_hi", [P, DC, D], F32R)
        wvo_lo = sb("wvo_lo", [P, DC, D], F32R)
        KQ_hi = sb("KQ_hi", [P, DC, KPAD], F32R)
        KQ_lo = sb("KQ_lo", [P, DC, KPAD], F32R)
        VO_sum = sb("VO_sum", [P, 3, D])
        VO_hi = sb("VO_hi", [P, KT, D], F32R)
        VO_lo = sb("VO_lo", [P, KT, D], F32R)
        key_bias = sb("key_bias", [P, KPAD])
        bk_col = sb("bk_col", [P, DC])
        bv_col = sb("bv_col", [P, DC])
        bo_row = sb("bo_row", [1, D])
        bq_wide = sb("bq_wide", [P, DC, P])
        bv_wide = sb("bv_wide", [P, DC, P])
        ones_row = sb("ones_row", [1, P])
        small = sb("small", [P, 5])
        bqwk_hi = sb("bqwk_hi", [P, DC, P], F32R)
        bqwk_lo = sb("bqwk_lo", [P, DC, P], F32R)
        vo_bias = sb("vo_bias", [P, D])
        gates = sb("gates", [P, 2])
        gate_tanh = sb("gate_tanh", [P, 2])
        ffn_scale = sb("ffn_scale", [P, 1])
        x_bn = sb("x_bn", [P, 2, 6])
        x_mv = sb("x_mv", [P, 2, 2])
        x_ve = sb("x_ve", [P, 2])
        x_rstd = sb("x_rstd", [P, 2])
        x_shift = sb("x_shift", [P, 2])
        minus_half = sb("minus_half", [P, TILES])
        xn = sb("xn", [P, 2, D])
        xnT_hi = sb("xnT_hi", [P, 2, DC, P], F32R)
        xnT_lo = sb("xnT_lo", [P, 2, DC, P], F32R)
        probs = sb("probs", [P, 2, KPAD])
        chunk_max = sb("chunk_max", [P, 2, 4])
        row_max = sb("row_max", [P, 2])
        exp_bias = sb("exp_bias", [P, 2])
        half_sum = sb("half_sum", [P, 2, 2])
        row_sum = sb("row_sum", [P, 1])
        row_inv = sb("row_inv", [P, 1])
        row_gain = sb("row_gain", [P, 1])
        pT_hi = sb("pT_hi", [P, KT, P], F32R)
        pT_lo = sb("pT_lo", [P, KT, P], F32R)
        resid = sb("resid", [P, D])
        z_bn = sb("z_bn", [P, 6])
        z_mv = sb("z_mv", [P, 2, 2])
        z_all = sb("z_all", [P, TILES * 2])
        z_ve = sb("z_ve", [P, TILES])
        z_rstd = sb("z_rstd", [P, TILES])
        z_negm = sb("z_negm", [P, TILES])
        z_shift = sb("z_shift", [P, TILES])
        w1 = sb("w1", [P, ET, D])
        w2 = sb("w2", [P, DC, E, R])
        wg = sb("wg", [E, D])
        bg_wide = sb("bg_wide", [P, E])
        w1T_hi = sb("w1T_hi", [P, DC, 2, UPW], F32R)
        w1T_lo = sb("w1T_lo", [P, DC, 2, UPW], F32R)
        w2T_hi = sb("w2T_hi", [P, ET, D], F32R)
        w2T_lo = sb("w2T_lo", [P, ET, D], F32R)
        ctx_flat = ctx_nat[:].rearrange("p n d -> p (n d)")
        hid = ctx_flat[:, 0:2 * ER].rearrange("p (b e r) -> p b e r", b=2, e=E)
        zb = ctx_flat[:, 2 * ER:2 * ER + 2 * D].rearrange("p (b d) -> p b d", b=2)

        def reuse(w):
            flat, b = w[:].rearrange("p a k -> p (a k)"), 2 * ER
            return (flat[:, 0:b].rearrange("p (b a n) -> p b a n", b=2, a=ET),
                    flat[:, b:b + 2 * D].rearrange("p (b a n) -> p b a n", b=2, a=DC))

        hT_hi, zT_hi = reuse(ctxT_hi)
        hT_lo, zT_lo = reuse(ctxT_lo)
        logits = sb("logits", [P, 2, E])
        top8 = sb("top8", [P, 2, 8])
        top_idx = sb("top_idx", [P, 2, 8], U32)
        top_diff = sb("top_diff", [P, 2])
        top_tanh = sb("top_tanh", [P, 2])
        top_gate = sb("top_gate", [P, 2, 2])
        expert_no = sb("expert_no", [P, E])
        half_signs = sb("half_signs", [P, 2])
        halves = sb("halves", [P, 2])
        is_top = sb("is_top", [P, 2, 2, E])
        gate_two = sb("gate_two", [P, 2, 2, E])
        expert_gate = sb("expert_gate", [P, 2, E])

        S = [bank(f"S{c}") for c in range(4)]
        T = [bank(f"T{c}") for c in range(2)]
        A = bank("A")
        B = bank("B")

        ld = {n: sem("ld_" + n) for n in ("wkq", "bq", "bk", "ctx0", "ctx1", "ctx2", "wo", "wv", "bvo", "gates",
                                          "x0", "x1", "w1", "w2", "wg")}
        s_ident0 = sem("ident_zero"); s_ident = sem("ident_ready")
        s_const = sem("constants_ready")
        s_gate = sem("gate_tanh_ready"); s_fscale = sem("ffn_scale_ready")
        s_wide = sem("wide_biases_ready")
        s_wkq_mm = sem("wkq_product"); s_wkq_hi = sem("wkq_hi_ready"); s_wkq_lo = sem("wkq_lo_ready")
        s_small_mm = sem("small_products"); s_small = sem("small_ready")
        s_bqwk_hi = sem("bqwk_hi_ready"); s_bqwk = sem("bqwk_ready")
        s_cT = sem("ctx_transposed"); s_cT_hi = sem("ctxT_hi_ready"); s_cT_lo = sem("ctxT_lo_ready")
        s_pad = sem("ctxT_pad_zero")
        s_kq_mm = sem("KQ_product"); s_kq_hi = sem("KQ_hi_ready"); s_kq_lo = sem("KQ_lo_ready")
        s_kb_mm = sem("key_bias_product"); s_kb = sem("key_bias_ready")
        s_woT_mm = sem("wo_transposed"); s_woT = sem("woT_ready"); s_woT_hi = sem("woT_hi_ready")
        s_woT_lo = sem("woT_lo_ready")
        s_wvo_mm = sem("wvo_product"); s_wvo_hi = sem("wvo_hi_ready"); s_wvo_lo = sem("wvo_lo_ready")
        s_vb_mm = sem("vo_bias_product"); s_vb = sem("vo_bias_ready")
        s_vo_mm = sem("VO_product"); s_vo_sum = sem("VO_sum_ready"); s_vo_hi = sem("VO_hi_ready")
        s_vo_lo = sem("VO_lo_ready")
        s_xbn = sem("x_bn_ready"); s_xmv = sem("x_mv_ready"); s_xve = sem("x_ve_ready")
        s_xpow = sem("x_rstd_ready"); s_xsh = sem("x_shift_ready")
        s_xn = sem("xn_ready"); s_xnT = sem("xn_transposed"); s_xnT_hi = sem("xnT_hi_ready")
        s_xnT_lo = sem("xnT_lo_ready")
        s_score = sem("scores_product"); s_biased = sem("scores_biased"); s_max = sem("row_max_ready")
        s_ebias = sem("exp_bias_ready"); s_exp = sem("probs_ready")
        s_pT = sem("probs_transposed"); s_pT_hi = sem("pT_hi_ready"); s_pT_lo = sem("pT_lo_ready")
        s_sum = sem("row_sum_ready"); s_inv = sem("row_inv_ready"); s_gain = sem("row_gain_ready")
        s_attn = sem("attention_product"); s_resid = sem("resid_ready"); s_x1 = sem("x1_ready")
        s_zbn = sem("z_bn_ready"); s_zmv = sem("z_mv_ready"); s_zall = sem("z_statistics_kept")
        s_w1T_mm = sem("w1_transposed"); s_w1T_hi = sem("w1T_hi_ready"); s_w1T_lo = sem("w1T_lo_ready")
        s_wgT_mm = sem("wg_transposed"); s_wgT_hi = sem("wgT_hi_ready"); s_wgT_lo = sem("wgT_lo_ready")
        s_w2T_mm = sem("w2_transposed"); s_w2T_hi = sem("w2T_hi_ready"); s_w2T_lo = sem("w2T_lo_ready")
        s_zve = sem("z_ve_ready"); s_zpow = sem("z_rstd_ready"); s_zneg = sem("z_negm_ready")
        s_zsh = sem("z_shift_ready")
        s_z = sem("z_ready"); s_zT = sem("z_transposed"); s_zT_hi = sem("zT_hi_ready")
        s_zT_lo = sem("zT_lo_ready")
        s_up = sem("up_product"); s_logit2 = sem("first_logits_ready"); s_logit = sem("last_logits_ready"); s_top = sem("top8_ready")
        s_idx = sem("top_idx_ready"); s_diff = sem("top_diff_ready"); s_ttanh = sem("top_tanh_ready")
        s_tgate = sem("top_gate_ready"); s_is = sem("is_top_ready"); s_two = sem("gate_two_ready")
        s_eg = sem("expert_gate_ready")
        s_gelu = sem("gelu_ready"); s_gated = sem("hidden_gated")
        s_hT = sem("hidden_transposed"); s_hT_hi = sem("hT_hi_ready"); s_hT_lo = sem("hT_lo_ready")
        s_down = sem("down_product"); s_final = sem("final_ready"); s_out = sem("out_stored")

        def f32(ap):
            return ap.bitcast(F32)

        def count(eng, value):
            return value if isinstance(value, int) else eng.compute_val(value)

        def tile_of(t):
            return X[:, bass.ds(t * D, D)]

        def VO_bank(n):
            return (T[0], T[1], A)[n % 3]

        def key_rows(n):
            return P if n < FULL else REST

        def ctxT_part(dst, g):
            n = 2 * P if g < 6 else REST
            return (dst[:, :, g * 2 * P:g * 2 * P + n],
                    S[g % 4][:].rearrange("p (a k) -> p a k", a=2)[:, :, 0:n])

        def pT_part(dst, g):
            tiles = GROUPS[g]
            rows = key_rows(tiles[-1])
            n = len(tiles)
            return (rows, dst[0:rows, tiles[0]:tiles[0] + n, :].rearrange("p a d -> p (a d)"),
                    T[g % 2][0:rows, 0:n * P])

        def wgT_part():
            return B[:, 0:DC * E].rearrange("p (a b n) -> p a b n", a=DC, b=2)

        block = ctx.enter_context(nc.Block())

        x_rows = x[0].rearrange("(p t) d -> p (t d)", t=TILES)
        out_rows = out[0].rearrange("(p t) d -> p (t d)", t=TILES)

        @block.sync
        def _(sp):
            full = ctx_1024[0, 0:FULL * P, :].rearrange("(p n) d -> p n d", n=FULL)
            third = FULL // 3
            for n in range(0, third, 2):
                sp.dma_start(ctx_nat[:, n:n + 2, :], full[:, n:n + 2, :]).then_inc(ld["ctx0"], 16)
            sp.dma_start(wk[:], Wk.rearrange("(a p) d -> p a d", p=P)).then_inc(ld["wkq"], 16)
            sp.dma_start(wq[:, :, 0:D], Wq.rearrange("(a p) d -> p a d", p=P)).then_inc(ld["wkq"], 16)
            sp.dma_start(ctx_nat[:, third:2 * third, :], full[:, third:2 * third, :]).then_inc(ld["ctx1"], 16)
            sp.dma_start(ctx_nat[:, 2 * third:FULL, :], full[:, 2 * third:FULL, :]).then_inc(ld["ctx2"], 16)
            sp.dma_start(ctx_nat[0:REST, FULL, :], ctx_1024[0, FULL * P:KEYS, :]).then_inc(ld["ctx2"], 16)
            sp.dma_start(wo[:], Wo.rearrange("(a p) d -> p a d", p=P)).then_inc(ld["wo"], 16)
            sp.dma_start(wv[:], Wv.rearrange("(a p) d -> p a d", p=P)).then_inc(ld["wv"], 16)
            for h in range(2):
                n = TILES // 2 * D
                sp.dma_start(X[:, h * n:(h + 1) * n], x_rows[:, h * n:(h + 1) * n]).then_inc(ld[f"x{h}"], 16)
            sp.dma_start(w1[:], W1.rearrange("e r d -> (e r) d").rearrange("(a p) d -> p a d", p=P)
                         ).then_inc(ld["w1"], 16)
            for dc in range(DC):
                sp.dma_start(w2[:, dc, :, :], W2[:, dc * P:(dc + 1) * P, :].rearrange("e p r -> p e r")
                             ).then_inc(ld["w2"], 16)
            for t in range(0, TILES, 2):
                sp.wait_ge(s_final, t + 2)
                sp.dma_start(out_rows[:, t * D:(t + 2) * D], X[:, t * D:(t + 2) * D]).then_inc(s_out, 16)
            sp.wait_ge(s_out, 16 * (TILES // 2))

        @block.gpsimd
        def _(pool):
            pool.memset(ident[:], 0.0).then_inc(s_ident0, 1)
            pool.wait_ge(s_ident0, 1)
            pool.affine_select(out=ident[:], in_=ident[:], compare_op=ALU.not_equal, fill=1.0, base=0,
                               pattern=[[-1, P]], channel_multiplier=1).then_inc(s_ident, 1)
            pool.memset(minus_half[:], -0.5).then_inc(s_const, 1)
            for e in range(E):
                pool.memset(expert_no[:, e:e + 1], float(e)).then_inc(s_const, 1)
            pool.memset(half_signs[:, 0:1], 0.5).then_inc(s_const, 1)
            pool.memset(half_signs[:, 1:2], -0.5).then_inc(s_const, 1)
            pool.memset(halves[:], 0.5).then_inc(s_const, 1)
            pool.memset(ones_row[:], 1.0).then_inc(s_const, 1)
            pool.wait_ge(s_const, E + 5)

            def x_moments(t, par):
                now, before = count(pool, t + 1), count(pool, t - 1)
                pool.wait_ge(s_const, E + 5)
                pool.wait_ge(s_xmv, now)
                if not isinstance(t, int) or t >= 2:
                    pool.wait_ge(s_xn, before)
                pool.tensor_scalar(x_ve[:, par:par + 1], x_mv[:, par, 1:2], EPS, None, ALU.add).then_inc(s_xve, 1)
                pool.wait_ge(s_xve, t + 1)
                pool.tensor_tensor(x_rstd[:, par:par + 1], x_ve[:, par:par + 1], minus_half[:, 0:1],
                                   ALU.pow).then_inc(s_xpow, 1)
                pool.wait_ge(s_const, E + 5)
                pool.wait_ge(s_xpow, now)
                pool.tensor_scalar(x_shift[:, par:par + 1], x_mv[:, par, 0:1], x_rstd[:, par:par + 1], -1.0,
                                   ALU.mult, ALU.mult).then_inc(s_xsh, 1)

            def vo_low(n):
                k = key_rows(n)
                pool.wait_ge(s_vo_hi, n + 1)
                pool.tensor_tensor(VO_lo[0:k, n, :], VO_sum[0:k, n % 3, :], f32(VO_hi[0:k, n, :]),
                                   ALU.subtract).then_inc(s_vo_lo, 1)

            for t in range(2):
                x_moments(t, t % 2)
            for n in range(KT):
                vo_low(n)
            x_moments(2, 0)

            def keep_z(t, par):
                pool.wait_ge(s_const, E + 5)
                pool.wait_ge(s_zmv, t + 1)
                pool.tensor_copy(z_all[:, bass.ds(t * 2, 2)], z_mv[:, par, :]).then_inc(s_zall, 1)

            x_moments(3, 1)
            with pool.Fori(0, TILES - 5, 2) as t:
                keep_z(t, 0)
                x_moments(t + 4, 0)
                keep_z(t + 1, 1)
                x_moments(t + 5, 1)

            def z_moments(t0, t1):
                batch = 1 if t0 == 0 else 2
                mean, var = (z_all[:].rearrange("p (t k) -> p t k", k=2)[:, t0:t1, k] for k in (0, 1))
                pool.wait_ge(s_zall, t1)
                pool.tensor_scalar(z_ve[:, t0:t1], var, EPS, None, ALU.add).then_inc(s_zve, 1)
                pool.wait_ge(s_zve, batch)
                pool.tensor_tensor(z_rstd[:, t0:t1], z_ve[:, t0:t1], minus_half[:, t0:t1], ALU.pow
                                   ).then_inc(s_zpow, 1)
                pool.tensor_scalar(z_negm[:, t0:t1], mean, -1.0, None, ALU.mult).then_inc(s_zneg, 1)
                pool.wait_ge(s_zneg, batch)
                pool.wait_ge(s_zpow, batch)
                pool.tensor_tensor(z_shift[:, t0:t1], z_negm[:, t0:t1], z_rstd[:, t0:t1], ALU.mult
                                   ).then_inc(s_zsh, 1)

            for t in range(TILES - 4, TILES - 2):
                keep_z(t, t % 2)
            z_moments(0, TILES - 2)
            for t in range(TILES - 2, TILES):
                keep_z(t, t % 2)
            z_moments(TILES - 2, TILES)

            def gate_hidden(t, par):
                pool.wait_ge(s_gelu, t + 1)
                pool.wait_ge(s_eg, t + 1)
                pool.tensor_tensor(hid[:, par], hid[:, par],
                                   expert_gate[:, par, :].unsqueeze(2).to_broadcast([P, E, R]),
                                   ALU.mult).then_inc(s_gated, 1)

            with pool.Fori(0, TILES - 1, 2) as t:
                gate_hidden(t, 0)
                gate_hidden(t + 1, 1)

        @block.tensor
        def _(pe):
            def three(dst, lhs_hi, lhs_lo, rhs_hi, rhs_lo, first, last):
                pe.matmul(dst, lhs_hi, rhs_hi, start=first, stop=False)
                pe.matmul(dst, lhs_hi, rhs_lo, start=False, stop=False)
                return pe.matmul(dst, lhs_lo, rhs_hi, start=False, stop=last)

            def transpose_ctx(g):
                piece, count_of = ((("ctx0", 32),) * 2 + (("ctx1", 16),) * 2 + (("ctx2", 32),) * 3)[g]
                pe.wait_ge(ld[piece], count_of)
                if g >= 4:
                    pe.wait_ge(s_cT_lo, g - 3)
                for jc in range(DC):
                    for n in [n for n in (2 * g, 2 * g + 1) if n < KT]:
                        k = key_rows(n)
                        at = jc * 2 * P + (n - 2 * g) * P
                        mm = pe.transpose(S[g % 4][:, at:at + k], ctx_nat[0:k, n, jc * P:(jc + 1) * P],
                                          ident[0:k, 0:k])
                mm.then_inc(s_cT, 1)

            pe.wait_ge(s_ident, 1)
            transpose_ctx(0)
            transpose_ctx(1)
            pe.wait_ge(ld["wkq"], 32)
            pe.wait_ge(ld["bq"], 16)
            for jc in range(DC):
                for cc in range(DC):
                    mm = pe.matmul(T[jc][:, 0:D + 1], wk[:, cc, jc * P:(jc + 1) * P], wq[:, cc, :],
                                   start=(cc == 0), stop=(cc == DC - 1))
                mm.then_inc(s_wkq_mm, 1)
            for g in range(2, 7):
                transpose_ctx(g)
            pe.wait_ge(ld["bk"], 16)
            pe.wait_ge(s_wide, 1)
            for i in range(DC + 1):
                for cc in range(DC):
                    w = wq[:, cc, i * P:(i + 1) * P] if i < DC else bq_wide[:, cc, :]
                    mm = pe.matmul(A[:, i:i + 1], w, bk_col[:, cc:cc + 1], start=(cc == 0), stop=(cc == DC - 1))
            mm.then_inc(s_small_mm, 1)
            pe.wait_ge(ld["wo"], 16)
            pe.wait_ge(s_wkq_lo, 2)
            pe.wait_ge(s_small, 2)
            for cc in range(DC):
                for oc in range(DC):
                    mm = pe.transpose(T[0][:, cc * D + oc * P:cc * D + (oc + 1) * P],
                                      wo[:, oc, cc * P:(cc + 1) * P], ident[:])
            mm.then_inc(s_woT_mm, 1)
            pe.wait_ge(s_wkq_hi, 2)
            pe.wait_ge(s_cT_hi, 7)
            pe.wait_ge(s_cT_lo, 7)
            pe.wait_ge(s_pad, 2)
            for u in range(DC * 4):
                fc, (k0, kn) = u // 4, CHUNKS[u % 4]
                if u >= 4:
                    pe.wait_ge(s_kq_lo, u - 3)
                for jc in range(DC):
                    mm = three(S[u % 4][:, 0:kn], wkq_hi[:, jc, fc * P:(fc + 1) * P],
                               wkq_lo[:, jc, fc * P:(fc + 1) * P], ctxT_hi[:, jc, k0:k0 + kn],
                               ctxT_lo[:, jc, k0:k0 + kn], jc == 0, jc == DC - 1)
                mm.then_inc(s_kq_mm, 1)
            def transpose_xn(t, par):
                pe.wait_ge(s_xn, t + 1)
                if not isinstance(t, int) or t >= 1:
                    pe.wait_ge(s_xnT_lo, t)
                for dc in range(DC):
                    mm = pe.transpose(B[:, dc * P:(dc + 1) * P], xn[:, par, dc * P:(dc + 1) * P], ident[:])
                mm.then_inc(s_xnT, 1)

            transpose_xn(0, 0)
            pe.wait_ge(s_woT, 1)
            pe.wait_ge(ld["wv"], 16)
            for jc in range(DC):
                for cc in range(DC):
                    mm = pe.matmul(T[1][:, jc * D:(jc + 1) * D], wv[:, cc, jc * P:(jc + 1) * P], woT[:, cc, :],
                                   start=(cc == 0), stop=(cc == DC - 1))
            mm.then_inc(s_wvo_mm, 1)
            pe.wait_ge(ld["bvo"], 32)
            pe.wait_ge(s_wide, 2)
            pe.wait_ge(s_const, E + 5)
            pe.wait_ge(s_small, 3)
            for cc in range(DC):
                pe.matmul(A[:, 0:D], bv_wide[:, cc, :], woT[:, cc, :], start=(cc == 0), stop=False)
            pe.matmul(A[:, 0:D], ones_row[:], bo_row[:], start=False, stop=True).then_inc(s_vb_mm, 1)
            pe.wait_ge(s_bqwk, 1)
            for c, (k0, kn) in enumerate(CHUNKS):
                pe.wait_ge(s_kq_lo, 5 + c)
                for jc in range(DC):
                    mm = three(S[c][:, 0:kn], bqwk_hi[:, jc, :], bqwk_lo[:, jc, :], ctxT_hi[:, jc, k0:k0 + kn],
                               ctxT_lo[:, jc, k0:k0 + kn], jc == 0, jc == DC - 1)
                mm.then_inc(s_kb_mm, 1)

            def turn(t, par, g, first=False):
                if g < 2:
                    pe.wait_ge(s_exp, t * 2 + (g + 1))
                if first and g == 0:
                    pe.wait_ge(s_vo_sum, KT)
                if not (first and g < 2):
                    pe.wait_ge(s_pT_lo, t * 4 + (g - 1))
                for n in GROUPS[g]:
                    k, at = key_rows(n), (n % 4) * P
                    mm = pe.transpose(T[g % 2][0:k, at:at + P], probs[:, par, n * P:n * P + k], ident[:])
                mm.then_inc(s_pT, 1)

            def scores(t, par, first=False, turns=True):
                pe.wait_ge(s_xnT_hi, t + 1)
                pe.wait_ge(s_xnT_lo, t + 1)
                if isinstance(t, int) and t == 1:
                    pe.wait_ge(s_w1T_lo, 2)
                    pe.wait_ge(s_w2T_lo, 2)
                for c, (k0, kn) in enumerate(CHUNKS):
                    if first:
                        pe.wait_ge(s_kb, c + 1)
                    else:
                        pe.wait_ge(s_biased, t * 4 + (c - 3))
                    for dc in range(DC):
                        mm = three(S[c][:, 0:kn], xnT_hi[:, par, dc, :], xnT_lo[:, par, dc, :],
                                   KQ_hi[:, dc, k0:k0 + kn], KQ_lo[:, dc, k0:k0 + kn], dc == 0, dc == DC - 1)
                    mm.then_inc(s_score, 1)
                    if not first:
                        turn(t - 1, 1 - par, c, first=isinstance(t, int) and t == 1)

            def project(t, par, first=False):
                if first:
                    pe.wait_ge(s_vo_sum, KT)
                else:
                    pe.wait_ge(s_x1, t)
                for dc in range(DC):
                    three(A[:, D:2 * D], xnT_hi[:, par, dc, :], xnT_lo[:, par, dc, :],
                          woT_hi[:, dc, :], woT_lo[:, dc, :], dc == 0, dc == DC - 1)

            def weigh(t, g):
                pe.wait_ge(s_pT_hi, t * 4 + (g + 1))
                pe.wait_ge(s_pT_lo, t * 4 + (g + 1))
                for n in GROUPS[g]:
                    k = key_rows(n)
                    mm = three(A[:, 0:D], pT_hi[0:k, n, :], pT_lo[0:k, n, :], VO_hi[0:k, n, :],
                               VO_lo[0:k, n, :], n == 0, n == KT - 1)
                if g == 3:
                    mm.then_inc(s_attn, 1)

            def attend(t, par, first=False, ahead=True):
                project(t, par, first)
                if first:
                    pe.wait_ge(s_wgT_lo, 1)
                if ahead:
                    transpose_xn(t + 2, par)
                for g in range(4):
                    if first:
                        pe.wait_ge(s_vo_lo, GROUPS[g][-1] + 1)
                    weigh(t, g)

            pe.wait_ge(s_kq_hi, 8)
            scores(0, 0, first=True)
            transpose_xn(1, 1)
            def transpose_w1():
                pe.wait_ge(ld["w1"], 16)
                pe.wait_ge(s_biased, 2)
                for dc in range(DC):
                    for et in range(ET):
                        mm = pe.transpose(S[dc][:, et * P:(et + 1) * P], w1[:, et, dc * P:(dc + 1) * P], ident[:])
                    mm.then_inc(s_w1T_mm, 1)

            def transpose_w2():
                pe.wait_ge(ld["w2"], 16 * DC)
                pe.wait_ge(s_biased, 4)
                for b in range(2):
                    for et in (2 * b, 2 * b + 1):
                        for dc in range(DC):
                            at = (et % 2) * D + dc * P
                            mm = pe.transpose(S[2 + b][:, at:at + P],
                                              w2[:, dc].rearrange("p e r -> p (e r)")[:, et * P:(et + 1) * P], ident[:])
                    mm.then_inc(s_w2T_mm, 1)

            def transpose_wg():
                pe.wait_ge(ld["wg"], 32)
                pe.wait_ge(s_xnT_lo, 2)
                for dc in range(DC):
                    mm = pe.transpose(B[:, dc * E:(dc + 1) * E], wg[:, dc * P:(dc + 1) * P], ident[0:E, 0:E])
                mm.then_inc(s_wgT_mm, 1)

            pe.wait_ge(s_wvo_hi, 1)
            pe.wait_ge(s_wvo_lo, 1)
            pe.wait_ge(s_woT_lo, 1)
            pe.wait_ge(s_vb, 1)
            for n in range(KT):
                k = key_rows(n)
                if n >= 3:
                    pe.wait_ge(s_vo_sum, n - 2)
                for jc in range(DC):
                    mm = three(VO_bank(n)[0:k, 0:D], ctxT_hi[:, jc, n * P:n * P + k],
                               ctxT_lo[:, jc, n * P:n * P + k], wvo_hi[:, jc, :], wvo_lo[:, jc, :],
                               jc == 0, jc == DC - 1)
                mm.then_inc(s_vo_mm, 1)
                if n == 2:
                    transpose_w1()
                elif n == 5:
                    transpose_w2()
                elif n == 8:
                    transpose_wg()

            pe.wait_ge(s_woT_hi, 1)
            for t in range(2):
                scores(t + 1, (t + 1) % 2)
                attend(t, t % 2, first=(t == 0))
            with pe.Fori(2, TILES - 3, 2) as t:
                for h in range(2):
                    scores(t + (h + 1), 1 - h)
                    attend(t + h, h)
            scores(TILES - 1, 1)
            attend(TILES - 2, 0, ahead=False)

            last = TILES - 1
            turn(last, 1, 0)
            turn(last, 1, 1)
            project(last, 1)
            turn(last, 1, 2)
            turn(last, 1, 3)
            weigh(last, 0)
            weigh(last, 1)

            def transpose_z(t, par, first=False):
                pe.wait_ge(s_z, t + 1)
                pe.wait_ge(s_xnT_lo, TILES) if first else pe.wait_ge(s_zT_lo, t)
                for dc in range(DC):
                    mm = pe.transpose(B[:, dc * P:(dc + 1) * P], zb[:, par, dc * P:(dc + 1) * P], ident[:])
                mm.then_inc(s_zT, 1)

            def up(t, par, first=False):
                pe.wait_ge(s_zT_hi, t + 1)
                pe.wait_ge(s_zT_lo, t + 1)
                if not first:
                    pe.wait_ge(s_gelu, t - 1)
                for b in range(2):
                    for dc in range(DC):
                        mm = three(S[2 * par + b][:, 0:UPW], zT_hi[:, par, dc, :], zT_lo[:, par, dc, :],
                                   w1T_hi[:, dc, b, :], w1T_lo[:, dc, b, :], dc == 0, dc == DC - 1)
                mm.then_inc(s_up, 1)

            def transpose_hidden(t, par, first=False):
                pe.wait_ge(s_gated, t + 1)
                if not first:
                    pe.wait_ge(s_hT_lo, t - 1)
                flat = hid[:, par].rearrange("p e r -> p (e r)")
                for et in range(ET):
                    mm = pe.transpose(T[par][:, et * P:(et + 1) * P], flat[:, et * P:(et + 1) * P], ident[:])
                mm.then_inc(s_hT, 1)

            def down(t, par, first=False):
                pe.wait_ge(s_hT_hi, t + 1)
                pe.wait_ge(s_hT_lo, t + 1)
                pe.wait_ge(s_x1, TILES) if first else pe.wait_ge(s_final, t)
                for et in range(ET):
                    mm = three(A[:, 0:D], hT_hi[:, par, et, :], hT_lo[:, par, et, :],
                               w2T_hi[:, et, :], w2T_lo[:, et, :], et == 0, et == ET - 1)
                mm.then_inc(s_down, 1)

            transpose_z(0, 0, first=True)
            weigh(last, 2)
            weigh(last, 3)
            pe.wait_ge(s_w1T_hi, 2)
            pe.wait_ge(s_w1T_lo, 2)
            pe.wait_ge(s_wgT_hi, 1)
            up(0, 0, first=True)
            transpose_z(1, 1)
            pe.wait_ge(s_w2T_hi, 2)
            pe.wait_ge(s_w2T_lo, 2)
            up(1, 1, first=True)
            transpose_z(2, 0)
            transpose_hidden(0, 0, first=True)
            up(2, 0)
            transpose_z(3, 1)
            transpose_hidden(1, 1, first=True)
            down(0, 0, first=True)
            up(3, 1)
            transpose_z(4, 0)
            transpose_hidden(2, 0)
            down(1, 1)
            with pe.Fori(4, TILES - 3, 2) as u:
                for h in range(2):
                    up(u + h, h)
                    transpose_z(u + (h + 1), 1 - h)
                    transpose_hidden(u + (h - 1), 1 - h)
                    down(u + (h - 2), h)
            up(TILES - 2, 0)
            transpose_z(TILES - 1, 1)
            transpose_hidden(TILES - 3, 1)
            down(TILES - 4, 0)
            up(TILES - 1, 1)
            transpose_hidden(TILES - 2, 0)
            down(TILES - 3, 1)
            down(TILES - 2, 0)
            transpose_hidden(TILES - 1, 1)
            down(TILES - 1, 1)

        @block.scalar
        def _(act):
            with nc.allow_non_contiguous_dma(reason="short vectors"):
                column = lambda v: v.rearrange("(a p) -> p a", p=P)
                row = lambda v: v.rearrange("(a d) -> a d", a=1)
                act.dma_start(wq[:, :, D], column(bq)).then_inc(ld["bq"], 16)
                act.dma_start(bk_col[:], column(bk)).then_inc(ld["bk"], 16)
                act.dma_start(bv_col[:], column(bv)).then_inc(ld["bvo"], 16)
                act.dma_start(bo_row[:], row(bo)).then_inc(ld["bvo"], 16)
                for n, g in enumerate((g_xattn, g_ffn)):
                    act.dma_start(gates[:, n:n + 1], row(g).to_broadcast([P, 1])).then_inc(ld["gates"], 16)
                act.dma_start(wg[:], Wg).then_inc(ld["wg"], 16)
                act.dma_start(bg_wide[:], row(bg).to_broadcast([P, E])).then_inc(ld["wg"], 16)
            act.preload_act_table(ACT.Exp)

            def ctx_high(g):
                act.wait_ge(s_cT, g + 1)
                act.activation(*ctxT_part(ctxT_hi, g), ACT.Copy).then_inc(s_cT_hi, 1)

            ctx_high(0)
            ctx_high(1)
            for jc in range(DC):
                act.wait_ge(s_wkq_mm, jc + 1)
                act.activation(wkq_hi[:, jc, :], T[jc][:, 0:D], ACT.Copy).then_inc(s_wkq_hi, 1)
            for g in range(2, 7):
                ctx_high(g)
            act.wait_ge(s_woT_mm, 1)
            flat = lambda w: w[:].rearrange("p a d -> p (a d)")
            act.activation(flat(woT), T[0][:], ACT.Copy).then_inc(s_woT, 1)
            act.activation(flat(woT_hi), T[0][:], ACT.Copy).then_inc(s_woT_hi, 1)
            def normalize_x(t, par):
                act.wait_ge(s_xsh, t + 1)
                if not isinstance(t, int) or t >= 2:
                    act.wait_ge(s_xnT, t - 1)
                act.activation(xn[:, par, :], tile_of(t), ACT.Identity, bias=x_shift[:, par:par + 1],
                               scale=x_rstd[:, par:par + 1]).then_inc(s_xn, 1)

            def xnT_high(t, par):
                act.wait_ge(s_xnT, t + 1)
                act.activation(xnT_hi[:, par].rearrange("p a d -> p (a d)"), B[:, 0:D], ACT.Copy
                               ).then_inc(s_xnT_hi, 1)

            act.wait_ge(s_small, 3)
            for u in range(DC * 4):
                fc, (k0, kn) = u // 4, CHUNKS[u % 4]
                act.wait_ge(s_kq_mm, u + 1)
                act.activation(KQ_hi[:, fc, k0:k0 + kn], S[u % 4][:, 0:kn], ACT.Identity,
                               bias=small[:, fc:fc + 1]).then_inc(s_kq_hi, 1)
                if u == 5:
                    act.wait_ge(ld["x0"], 16)
                    normalize_x(0, 0)
            xnT_high(0, 0)
            normalize_x(1, 1)
            act.wait_ge(s_wvo_mm, 1)
            act.activation(flat(wvo_hi), T[1][:], ACT.Copy).then_inc(s_wvo_hi, 1)
            act.wait_ge(s_vb_mm, 1)
            act.activation(vo_bias[:], A[:, 0:D], ACT.Copy).then_inc(s_vb, 1)
            act.wait_ge(ld["gates"], 32)
            act.activation(gate_tanh[:], gates[:], ACT.Tanh).then_inc(s_gate, 1)

            def exponentials(t, par, h):
                if h == 0:
                    act.wait_ge(s_ebias, t + 1)
                    if not isinstance(t, int) or t >= 2:
                        act.wait_ge(s_sum, t - 1)
                cut = slice(0, HALF) if h == 0 else slice(HALF, KEYS)
                act.activation(probs[:, par, cut], probs[:, par, cut], ACT.Exp, bias=exp_bias[:, par:par + 1],
                               scale=SCALE, accum_out=half_sum[:, par, h:h + 1]).then_inc(s_exp, 1)

            def pT_high(t, g):
                act.wait_ge(s_pT, t * 4 + (g + 1))
                rows, dst, src = pT_part(pT_hi, g)
                act.activation(dst, src, ACT.Copy).then_inc(s_pT_hi, 1)

            def w1T_high():
                for dc in range(DC):
                    act.wait_ge(s_w1T_mm, dc + 1)
                    act.activation(w1T_hi[:, dc, :, 0:ER // 2], S[dc][:].rearrange("p (b n) -> p b n", b=2), ACT.Copy
                                   ).then_inc(s_w1T_hi, 1)

            def w2T_high():
                for b in range(2):
                    act.wait_ge(s_w2T_mm, b + 1)
                    act.activation(w2T_hi[:, 2 * b:2 * b + 2, :].rearrange("p a d -> p (a d)"), S[2 + b][:],
                                   ACT.Copy).then_inc(s_w2T_hi, 1)

            def wgT_high():
                act.wait_ge(s_wgT_mm, 1)
                act.activation(w1T_hi[:, :, :, ER // 2:UPW], wgT_part(), ACT.Copy).then_inc(s_wgT_hi, 1)

            for n in range(KT):
                k = key_rows(n)
                act.wait_ge(s_vo_sum, n + 1)
                act.activation(VO_hi[0:k, n, :], VO_sum[0:k, n % 3, :], ACT.Copy).then_inc(s_vo_hi, 1)
                if n == 1:
                    xnT_high(1, 1)
                if n in (2, 5, 8):
                    (w1T_high, w2T_high, wgT_high)[n // 3]()
                if n in (3, 7):
                    exponentials(0, 0, n // 7)

            def step(t, par, ahead=True, two_ahead=True):
                pT_high(t, 0)
                if two_ahead:
                    normalize_x(t + 2, par)
                for g in range(1, 4):
                    pT_high(t, g)
                if ahead:
                    exponentials(t + 1, 1 - par, 0)
                    exponentials(t + 1, 1 - par, 1)
                if two_ahead:
                    xnT_high(t + 2, par)

            act.wait_ge(ld["x1"], 16)
            step(0, 0)
            step(1, 1)
            with act.Fori(2, TILES - 3, 2) as t:
                step(t, 0)
                step(t + 1, 1)
            step(TILES - 2, 0, two_ahead=False)
            act.preload_act_table(ACT.Gelu)
            step(TILES - 1, 1, ahead=False, two_ahead=False)

            def normalize_z(t, par):
                if not isinstance(t, int) or t >= 2:
                    act.wait_ge(s_zT, t - 1)
                act.activation(zb[:, par, :], tile_of(t), ACT.Identity, bias=z_shift[:, bass.ds(t, 1)],
                               scale=z_rstd[:, bass.ds(t, 1)]).then_inc(s_z, 1)

            def zT_high(t, par):
                act.wait_ge(s_zT, t + 1)
                act.activation(zT_hi[:, par].rearrange("p a d -> p (a d)"), B[:, 0:D], ACT.Copy
                               ).then_inc(s_zT_hi, 1)

            def gelu(t, par):
                act.wait_ge(s_logit, t + 1)
                if not isinstance(t, int) or t >= 2:
                    act.wait_ge(s_hT, t - 1)
                for b in range(2):
                    ins = act.activation(hid[:, par].rearrange("p (b e) r -> p b (e r)", b=2)[:, b, :],
                                         S[2 * par + b][:, 0:ER // 2], ACT.Gelu)
                    if b == 1:
                        ins.then_inc(s_gelu, 1)

            def gate_of_two(t, par):
                act.wait_ge(s_diff, t + 1)
                act.activation(top_tanh[:, par:par + 1], top_diff[:, par:par + 1], ACT.Tanh, scale=0.5
                               ).then_inc(s_ttanh, 1)

            def hT_high(t, par):
                act.wait_ge(s_hT, t + 1)
                act.activation(hT_hi[:, par].rearrange("p a d -> p (a d)"), T[par][:], ACT.Copy
                               ).then_inc(s_hT_hi, 1)

            act.wait_ge(s_zsh, 1)
            normalize_z(0, 0)
            normalize_z(1, 1)
            zT_high(0, 0)

            def step2(u, par, z1=True, hidden=True, z2=True):
                if z1:
                    zT_high(u + 1, 1 - par)
                gelu(u, par)
                gate_of_two(u, par)
                if hidden:
                    hT_high(u - 1, 1 - par)
                if z2:
                    normalize_z(u + 2, par)

            step2(0, 0, hidden=False)
            step2(1, 1)
            step2(2, 0)
            step2(3, 1)
            act.wait_ge(s_zsh, 2)
            with act.Fori(4, TILES - 3, 2) as u:
                step2(u, 0)
                step2(u + 1, 1)
            step2(TILES - 2, 0, z2=False)
            step2(TILES - 1, 1, z1=False, z2=False)
            hT_high(TILES - 1, 1)

        @block.vector
        def _(dve):
            dve.memset(f32(ctxT_hi[:, :, KEYS:KPAD]), 0.0).then_inc(s_pad, 1)
            dve.memset(f32(ctxT_lo[:, :, KEYS:KPAD]), 0.0).then_inc(s_pad, 1)
            dve.wait_ge(ld["bq"], 16)
            dve.tensor_copy(bq_wide[:], wq[:, :, D:D + 1].to_broadcast([P, DC, P])).then_inc(s_wide, 1)

            def ctx_low(g):
                dve.wait_ge(s_cT_hi, g + 1)
                dst, src = ctxT_part(ctxT_lo, g)
                dve.tensor_tensor(dst, src, f32(ctxT_part(ctxT_hi, g)[0]), ALU.subtract).then_inc(s_cT_lo, 1)

            ctx_low(0)
            ctx_low(1)
            for jc in range(DC):
                dve.wait_ge(s_wkq_hi, jc + 1)
                dve.tensor_copy(small[:, 3 + jc:4 + jc], T[jc][:, D:D + 1]).then_inc(s_small, 1)
                dve.tensor_tensor(wkq_lo[:, jc, :], T[jc][:, 0:D], f32(wkq_hi[:, jc, :]), ALU.subtract
                                  ).then_inc(s_wkq_lo, 1)
            for g in range(2, 7):
                ctx_low(g)
            dve.wait_ge(s_small, 2)
            wide = small[:, 3:5].unsqueeze(2).to_broadcast([P, DC, P])
            dve.tensor_copy(bqwk_hi[:], wide).then_inc(s_bqwk_hi, 1)
            dve.wait_ge(s_small_mm, 1)
            dve.tensor_copy(small[:, 0:3], A[:, 0:3]).then_inc(s_small, 1)
            dve.wait_ge(s_bqwk_hi, 1)
            dve.tensor_tensor(bqwk_lo[:], wide, f32(bqwk_hi[:]), ALU.subtract).then_inc(s_bqwk, 1)
            dve.wait_ge(ld["bvo"], 32)
            dve.tensor_copy(bv_wide[:], bv_col[:].unsqueeze(2).to_broadcast([P, DC, P])).then_inc(s_wide, 1)
            dve.wait_ge(s_small, 3)
            dve.wait_ge(s_woT_hi, 1)
            flat = lambda w: w[:].rearrange("p a d -> p (a d)")
            dve.tensor_tensor(flat(woT_lo), T[0][:], f32(flat(woT_hi)), ALU.subtract).then_inc(s_woT_lo, 1)
            def x_statistics(t, par):
                now, before = count(dve, t + 1), count(dve, t - 1)
                dve.wait_ge(ld["x0"], 16)
                if not isinstance(t, int) or t >= 2:
                    dve.wait_ge(s_xsh, before)
                dve.bn_stats(x_bn[:, par, :], tile_of(t)).then_inc(s_xbn, 1)
                dve.wait_ge(ld["x0"], 16)
                dve.wait_ge(s_xbn, now)
                dve.bn_aggr(x_mv[:, par, :], x_bn[:, par, :]).then_inc(s_xmv, 1)

            def xnT_low(t, par):
                dve.wait_ge(s_xnT_hi, t + 1)
                dst, hi = (w[:, par].rearrange("p a d -> p (a d)") for w in (xnT_lo, xnT_hi))
                dve.tensor_tensor(dst, B[:, 0:D], f32(hi), ALU.subtract).then_inc(s_xnT_lo, 1)

            for u in range(DC * 4):
                fc, (k0, kn) = u // 4, CHUNKS[u % 4]
                dve.wait_ge(s_kq_hi, u + 1)
                dve.scalar_tensor_tensor(out=KQ_lo[:, fc, k0:k0 + kn], in0=S[u % 4][:, 0:kn],
                                         scalar=small[:, fc:fc + 1], in1=f32(KQ_hi[:, fc, k0:k0 + kn]),
                                         op0=ALU.add, op1=ALU.subtract).then_inc(s_kq_lo, 1)
                if u == 1:
                    dve.wait_ge(ld["x0"], 16)
                    x_statistics(0, 0)
                    x_statistics(1, 1)
            xnT_low(0, 0)
            dve.wait_ge(s_wvo_hi, 1)
            dve.tensor_tensor(flat(wvo_lo), T[1][:], f32(flat(wvo_hi)), ALU.subtract).then_inc(s_wvo_lo, 1)

            for c, (k0, kn) in enumerate(CHUNKS):
                dve.wait_ge(s_kb_mm, c + 1)
                dve.tensor_scalar(key_bias[:, k0:k0 + kn], S[c][:, 0:kn], small[:, 2:3], None, ALU.add
                                  ).then_inc(s_kb, 1)
            dve.wait_ge(s_kb, 4)


            def biased(t, par, c):
                if c == 0 and (not isinstance(t, int) or t >= 2):
                    dve.wait_ge(s_pT, t * 4 - 4)
                k0, kn = CHUNKS[c]
                n = min(kn, KEYS - k0)
                now = count(dve, t * 4 + (c + 1))
                dve.wait_ge(s_kb, 4)
                dve.wait_ge(s_score, now)
                dve.tensor_tensor_reduce(
                    out=probs[:, par, k0:k0 + n], in0=S[c][:, 0:n], in1=key_bias[:, k0:k0 + n], scale=1.0,
                    scalar=-3.0e38, op0=ALU.add, op1=ALU.max, accum_out=chunk_max[:, par, c:c + 1]
                ).then_inc(s_biased, 1)

            def maximum(t, par):
                dve.wait_ge(s_biased, t * 4 + 4)
                dve.reduce_max(row_max[:, par:par + 1], chunk_max[:, par, :], AX_X).then_inc(s_max, 1)
                dve.wait_ge(s_max, t + 1)
                dve.tensor_scalar(exp_bias[:, par:par + 1], row_max[:, par:par + 1], -SCALE, None, ALU.mult
                                  ).then_inc(s_ebias, 1)

            def pT_low(t, g):
                dve.wait_ge(s_pT_hi, t * 4 + (g + 1))
                rows, dst, src = pT_part(pT_lo, g)
                dve.tensor_tensor(dst, src, f32(pT_part(pT_hi, g)[1]), ALU.subtract).then_inc(s_pT_lo, 1)

            def row_gains(t, par):
                dve.wait_ge(s_exp, t * 2 + 2)
                if not isinstance(t, int) or t >= 1:
                    dve.wait_ge(s_inv, t)
                dve.tensor_tensor(row_sum[:], half_sum[:, par, 0:1], half_sum[:, par, 1:2], ALU.add
                                  ).then_inc(s_sum, 1)
                dve.wait_ge(s_sum, t + 1)
                if not isinstance(t, int) or t >= 1:
                    dve.wait_ge(s_gain, t)
                dve.reciprocal(row_inv[:], row_sum[:]).then_inc(s_inv, 1)
                dve.wait_ge(s_inv, t + 1)
                if not isinstance(t, int) or t >= 1:
                    dve.wait_ge(s_x1, t)
                dve.tensor_scalar(row_gain[:], row_inv[:], gate_tanh[:, 0:1], None, ALU.mult).then_inc(s_gain, 1)

            def attention_out(t):
                dve.wait_ge(s_attn, t + 1)
                dve.scalar_tensor_tensor(out=resid[:], in0=A[:, D:2 * D], scalar=gate_tanh[:, 0:1], in1=tile_of(t),
                                         op0=ALU.mult, op1=ALU.add).then_inc(s_resid, 1)
                dve.wait_ge(s_resid, t + 1)
                dve.wait_ge(s_gain, t + 1)
                dve.scalar_tensor_tensor(out=tile_of(t), in0=A[:, 0:D], scalar=row_gain[:], in1=resid[:],
                                         op0=ALU.mult, op1=ALU.add).then_inc(s_x1, 1)

            def z_statistics(t, par):
                dve.wait_ge(ld["x1"], 16)
                dve.wait_ge(s_x1, t + 1)
                if not isinstance(t, int) or t >= 1:
                    dve.wait_ge(s_zmv, t)
                dve.bn_stats(z_bn[:], tile_of(t)).then_inc(s_zbn, 1)
                now, before = count(dve, t + 1), count(dve, t - 1)
                dve.wait_ge(ld["x1"], 16)
                dve.wait_ge(s_zbn, now)
                if not isinstance(t, int) or t >= 2:
                    dve.wait_ge(s_zall, before)
                dve.bn_aggr(z_mv[:, par, :], z_bn[:]).then_inc(s_zmv, 1)

            dve.wait_ge(s_gate, 1)
            dve.tensor_scalar(ffn_scale[:], gate_tanh[:, 1:2], LORA_SCALING, None, ALU.mult).then_inc(s_fscale, 1)
            for c in range(4):
                biased(0, 0, c)
            maximum(0, 0)

            def w1T_low():
                for dc in range(DC):
                    dve.wait_ge(s_w1T_hi, dc + 1)
                    dve.tensor_tensor(w1T_lo[:, dc, :, 0:ER // 2], S[dc][:].rearrange("p (b n) -> p b n", b=2),
                                      f32(w1T_hi[:, dc, :, 0:ER // 2]), ALU.subtract).then_inc(s_w1T_lo, 1)

            def w2T_low():
                for b in range(2):
                    dve.wait_ge(s_w2T_hi, b + 1)
                    dst, hi = (w[:, 2 * b:2 * b + 2, :].rearrange("p a d -> p (a d)") for w in (w2T_lo, w2T_hi))
                    dve.tensor_tensor(dst, S[2 + b][:], f32(hi), ALU.subtract).then_inc(s_w2T_lo, 1)

            def wgT_low():
                dve.wait_ge(s_wgT_hi, 1)
                dve.tensor_tensor(w1T_lo[:, :, :, ER // 2:UPW], wgT_part(), f32(w1T_hi[:, :, :, ER // 2:UPW]),
                                  ALU.subtract).then_inc(s_wgT_lo, 1)

            dve.wait_ge(s_vb, 1)
            for n in range(KT):
                k = key_rows(n)
                dve.wait_ge(s_vo_mm, n + 1)
                if n >= 3:
                    dve.wait_ge(s_vo_lo, n - 2)
                dve.tensor_tensor(VO_sum[0:k, n % 3, :], VO_bank(n)[0:k, 0:D], vo_bias[0:k, :], ALU.add
                                  ).then_inc(s_vo_sum, 1)
                if n == 1:
                    xnT_low(1, 1)
                if n in (3, 6, 9):
                    (w1T_low, w2T_low, wgT_low)[n // 3 - 1]()
            x_statistics(2, 0)
            dve.wait_ge(ld["x1"], 16)

            def step(t, par, before=True, ahead=True, two_ahead=True, three_ahead=True):
                if before:
                    attention_out(t - 1)
                if ahead:
                    biased(t + 1, 1 - par, 0)
                if before:
                    z_statistics(t - 1, 1 - par)
                pT_low(t, 0)
                if ahead:
                    biased(t + 1, 1 - par, 1)
                row_gains(t, par)
                pT_low(t, 1)
                if ahead:
                    biased(t + 1, 1 - par, 2)
                pT_low(t, 2)
                if three_ahead:
                    x_statistics(t + 3, 1 - par)
                if ahead:
                    biased(t + 1, 1 - par, 3)
                    maximum(t + 1, 1 - par)
                pT_low(t, 3)
                if two_ahead:
                    xnT_low(t + 2, par)

            step(0, 0, before=False)
            step(1, 1)
            with dve.Fori(2, TILES - 5, 2) as t:
                step(t, 0)
                step(t + 1, 1)
            step(TILES - 4, 0)
            step(TILES - 3, 1, three_ahead=False)
            step(TILES - 2, 0, two_ahead=False, three_ahead=False)
            step(TILES - 1, 1, ahead=False, two_ahead=False, three_ahead=False)

            def zT_low(t, par):
                dve.wait_ge(s_zT_hi, t + 1)
                dst, hi = (w[:, par].rearrange("p a d -> p (a d)") for w in (zT_lo, zT_hi))
                dve.tensor_tensor(dst, B[:, 0:D], f32(hi), ALU.subtract).then_inc(s_zT_lo, 1)

            def route(t, par):
                n = E // 2
                dve.wait_ge(s_up, t + 1)
                if not isinstance(t, int) or t >= 2:
                    dve.wait_ge(s_eg, t - 1)
                for b in range(2):
                    ins = dve.tensor_tensor(logits[:, par, b * n:(b + 1) * n], S[2 * par + b][:, ER // 2:UPW],
                                            bg_wide[:, b * n:(b + 1) * n], ALU.add)
                    ins.then_inc(s_logit2 if b == 0 else s_logit, 1)
                dve.wait_ge(ld["wg"], 32)
                dve.wait_ge(s_logit2, t + 1)
                dve.wait_ge(s_logit, t + 1)
                dve.max(top8[:, par, :], logits[:, par, :]).then_inc(s_top, 1)
                dve.wait_ge(ld["wg"], 32)
                dve.wait_ge(s_top, t + 1)
                dve.max_index(top_idx[:, par, :], top8[:, par, :], logits[:, par, :]).then_inc(s_idx, 1)
                dve.tensor_tensor(top_diff[:, par:par + 1], top8[:, par, 0:1], top8[:, par, 1:2], ALU.subtract
                                  ).then_inc(s_diff, 1)

            def spread_gates(t, par):
                dve.wait_ge(s_ttanh, t + 1)
                dve.scalar_tensor_tensor(out=top_gate[:, par, :], in0=half_signs[:], scalar=top_tanh[:, par:par + 1],
                                         in1=halves[:], op0=ALU.mult, op1=ALU.add).then_inc(s_tgate, 1)
                dve.wait_ge(s_idx, t + 1)
                dve.tensor_tensor(is_top[:, par], expert_no[:].unsqueeze(1).to_broadcast([P, 2, E]),
                                  top_idx[:, par, 0:2].unsqueeze(2).to_broadcast([P, 2, E]), ALU.is_equal
                                  ).then_inc(s_is, 1)
                dve.wait_ge(s_tgate, t + 1)
                dve.wait_ge(s_is, t + 1)
                dve.tensor_tensor(gate_two[:, par], is_top[:, par],
                                  top_gate[:, par, :].unsqueeze(2).to_broadcast([P, 2, E]), ALU.mult
                                  ).then_inc(s_two, 1)
                dve.wait_ge(s_two, t + 1)
                if not isinstance(t, int) or t >= 2:
                    dve.wait_ge(s_gated, t - 1)
                dve.tensor_tensor(expert_gate[:, par, :], gate_two[:, par, 0, :], gate_two[:, par, 1, :], ALU.add
                                  ).then_inc(s_eg, 1)

            def hT_low(t, par):
                dve.wait_ge(s_hT_hi, t + 1)
                dst, hi = (w[:, par].rearrange("p a d -> p (a d)") for w in (hT_lo, hT_hi))
                dve.tensor_tensor(dst, T[par][:], f32(hi), ALU.subtract).then_inc(s_hT_lo, 1)

            def finish(t):
                dve.wait_ge(s_down, t + 1)
                dve.scalar_tensor_tensor(out=tile_of(t), in0=A[:, 0:D], scalar=ffn_scale[:], in1=tile_of(t),
                                         op0=ALU.mult, op1=ALU.add).then_inc(s_final, 1)

            dve.wait_ge(s_const, E + 5)
            dve.wait_ge(s_fscale, 1)
            dve.wait_ge(ld["wg"], 32)
            zT_low(0, 0)
            attention_out(TILES - 1)
            z_statistics(TILES - 1, 1)

            def step2(u, par, z1=True, hidden=True, last=True):
                route(u, par)
                if z1:
                    zT_low(u + 1, 1 - par)
                spread_gates(u, par)
                if hidden:
                    hT_low(u - 1, 1 - par)
                if last:
                    finish(u - 2)

            step2(0, 0, hidden=False, last=False)
            step2(1, 1, last=False)
            step2(2, 0)
            step2(3, 1)
            with dve.Fori(4, TILES - 3, 2) as u:
                step2(u, 0)
                step2(u + 1, 1)
            step2(TILES - 2, 0)
            step2(TILES - 1, 1, z1=False)
            finish(TILES - 2)
            hT_low(TILES - 1, 1)
            finish(TILES - 1)


_INS = ["x", "ctx_1024", "g_xattn", "g_ffn", "L0_xattn_Wq", "L0_xattn_bq", "L0_xattn_Wk", "L0_xattn_bk",
        "L0_xattn_Wv", "L0_xattn_bv", "L0_xattn_Wo", "L0_xattn_bo", "L0_ffn_Wg", "L0_ffn_bg", "L0_ffn_W1",
        "L0_ffn_W2"]


def kernel(**inputs):
    import numpy as _np
    import concourse.bacc as _bacc
    from concourse import mybir as _mybir
    from concourse.bass_utils import run_bass_kernel_spmd as _run

    nc = _bacc.Bacc("TRN2", target_bir_lowering=False, num_devices=1)
    arrays, args = {}, []
    for name in _INS:
        a = _np.ascontiguousarray(inputs[name])
        arrays[f"in_{name}"] = a
        args.append(nc.dram_tensor(f"in_{name}", a.shape, _mybir.dt.from_np(a.dtype), kind="ExternalInput").ap())
    shape = tuple(inputs["x"].shape)
    args.append(nc.dram_tensor("out_0", shape, _mybir.dt.float32, kind="ExternalOutput").ap())
    flamingo_layer(nc, *args)
    r = _run(nc, [arrays], core_ids=[0])
    return r.results[0]["out_0"]
```

```python
from contextlib import ExitStack

import concourse.bass as bass
from concourse import mybir

ALU = mybir.AluOpType
ACT = mybir.ActivationFunctionType
AX_X = mybir.AxisListType.X
F32 = mybir.dt.float32
F32R = mybir.dt.float32r
U32 = mybir.dt.uint32

P = 128
EPS = 1e-5
LORA_SCALING = 2.0


def flamingo_layer(nc, x, ctx_1024, g_xattn, g_ffn, Wq, bq, Wk, bk, Wv, bv, Wo, bo, Wg, bg, W1, W2, out):
    SQ, D = x.shape[1], x.shape[2]
    KEYS = ctx_1024.shape[1]
    E, R, _ = W1.shape
    TILES = SQ // P
    DC = D // P
    FULL = KEYS // P
    REST = KEYS - FULL * P
    KT = FULL + 1
    KPAD = KEYS + KEYS % 2
    CH = 402
    CHUNKS = [(c * CH, min(CH, KPAD - c * CH)) for c in range(4)]
    GROUPS = [range(g * 4, min(g * 4 + 4, KT)) for g in range(4)]
    HALF = 2 * CH
    ER = E * R
    ET = ER // P
    UPW = ER // 2 + E // 2
    SCALE = float(D) ** -0.5
    WARM_UP = 7
    assert D == 2 * P and REST > 0 and CHUNKS[-1][0] + CHUNKS[-1][1] == KPAD and ER == 512
    assert TILES % 2 == 0 and TILES >= 8

    with ExitStack() as ctx:
        def sb(name, shape, dt=F32):
            return ctx.enter_context(nc.sbuf_tensor(name, shape, dt))

        def bank(name):
            return ctx.enter_context(nc.psum_tensor(name, [P, 512], F32))

        def sem(name):
            return ctx.enter_context(nc.semaphore(name))

        X = sb("X", [P, TILES * D])
        ident = sb("ident", [P, P])
        warm = sb("warm", [P, P])
        ctx_nat = sb("ctx_nat", [P, KT, D])
        ctxT_hi = sb("ctxT_hi", [P, DC, KPAD], F32R)
        ctxT_lo = sb("ctxT_lo", [P, DC, KPAD], F32R)
        wq = sb("wq", [P, DC, D + 1])
        wk = sb("wk", [P, DC, D])
        wv = sb("wv", [P, DC, D])
        wo = sb("wo", [P, DC, D])
        woT = sb("woT", [P, DC, D])
        woT_hi = sb("woT_hi", [P, DC, D], F32R)
        woT_lo = sb("woT_lo", [P, DC, D], F32R)
        wkq_hi = sb("wkq_hi", [P, DC, D], F32R)
        wkq_lo = sb("wkq_lo", [P, DC, D], F32R)
        wvo_hi = sb("wvo_hi", [P, DC, D], F32R)
        wvo_lo = sb("wvo_lo", [P, DC, D], F32R)
        KQ_hi = sb("KQ_hi", [P, DC, KPAD], F32R)
        KQ_lo = sb("KQ_lo", [P, DC, KPAD], F32R)
        VO_sum = sb("VO_sum", [P, 3, D])
        VO_hi = sb("VO_hi", [P, KT, D], F32R)
        VO_lo = sb("VO_lo", [P, KT, D], F32R)
        key_bias = sb("key_bias", [P, KPAD])
        bk_col = sb("bk_col", [P, DC])
        bv_col = sb("bv_col", [P, DC])
        bo_row = sb("bo_row", [1, D])
        bq_wide = sb("bq_wide", [P, DC, P])
        bv_wide = sb("bv_wide", [P, DC, P])
        ones_row = sb("ones_row", [1, P])
        small = sb("small", [P, 5])
        bqwk_row = sb("bqwk_row", [P, D])
        bqwk_used = sb("bqwk_used", [P, 2, D])
        kb_col = sb("kb_col", [P, KT])
        vo_bias = sb("vo_bias", [P, D])
        gates = sb("gates", [P, 2])
        gate_tanh = sb("gate_tanh", [P, 2])
        ffn_scale = sb("ffn_scale", [P, 1])
        x_bn = sb("x_bn", [P, 2, 6])
        x_mv = sb("x_mv", [P, 2, 2])
        x_ve = sb("x_ve", [P, 2])
        x_rstd = sb("x_rstd", [P, 2])
        x_shift = sb("x_shift", [P, 2])
        minus_half = sb("minus_half", [P, TILES])
        xn = sb("xn", [P, 2, D])
        xnT_hi = sb("xnT_hi", [P, 2, DC, P], F32R)
        xnT_lo = sb("xnT_lo", [P, 2, DC, P], F32R)
        probs = sb("probs", [P, 2, KPAD])
        chunk_max = sb("chunk_max", [P, 2, 4])
        row_max = sb("row_max", [P, 2])
        exp_bias = sb("exp_bias", [P, 2])
        half_sum = sb("half_sum", [P, 2, 2])
        row_sum = sb("row_sum", [P, 1])
        row_inv = sb("row_inv", [P, 1])
        row_gain = sb("row_gain", [P, 1])
        pT_hi = sb("pT_hi", [P, KT, P], F32R)
        pT_lo = sb("pT_lo", [P, KT, P], F32R)
        resid = sb("resid", [P, D])
        z_bn = sb("z_bn", [P, 6])
        z_mv = sb("z_mv", [P, 2, 2])
        z_all = sb("z_all", [P, TILES * 2])
        z_ve = sb("z_ve", [P, TILES])
        z_rstd = sb("z_rstd", [P, TILES])
        z_negm = sb("z_negm", [P, TILES])
        z_shift = sb("z_shift", [P, TILES])
        w1 = sb("w1", [P, ET, D])
        w2 = sb("w2", [P, DC, E, R])
        wg = sb("wg", [E, D])
        bg_wide = sb("bg_wide", [P, E])
        w1T_hi = sb("w1T_hi", [P, DC, 2, UPW], F32R)
        w1T_lo = sb("w1T_lo", [P, DC, 2, UPW], F32R)
        w2T_hi = sb("w2T_hi", [P, ET, D], F32R)
        w2T_lo = sb("w2T_lo", [P, ET, D], F32R)
        ctx_flat = ctx_nat[:].rearrange("p n d -> p (n d)")
        hid = ctx_flat[:, 0:2 * ER].rearrange("p (b e r) -> p b e r", b=2, e=E)
        zb = ctx_flat[:, 2 * ER:2 * ER + 2 * D].rearrange("p (b d) -> p b d", b=2)

        def reuse(w):
            flat, b = w[:].rearrange("p a k -> p (a k)"), 2 * ER
            return (flat[:, 0:b].rearrange("p (b a n) -> p b a n", b=2, a=ET),
                    flat[:, b:b + 2 * D].rearrange("p (b a n) -> p b a n", b=2, a=DC))

        hT_hi, zT_hi = reuse(ctxT_hi)
        hT_lo, zT_lo = reuse(ctxT_lo)
        logits = sb("logits", [P, 2, E])
        top8 = sb("top8", [P, 2, 8])
        top_idx = sb("top_idx", [P, 2, 8], U32)
        top_diff = sb("top_diff", [P, 2])
        top_tanh = sb("top_tanh", [P, 2])
        top_gate = sb("top_gate", [P, 2, 2])
        expert_no = sb("expert_no", [P, E])
        half_signs = sb("half_signs", [P, 2])
        halves = sb("halves", [P, 2])
        is_top = sb("is_top", [P, 2, 2, E])
        gate_two = sb("gate_two", [P, 2, 2, E])
        expert_gate = sb("expert_gate", [P, 2, E])

        S = [bank(f"S{c}") for c in range(4)]
        T = [bank(f"T{c}") for c in range(2)]
        A = bank("A")
        B = bank("B")

        ld = {n: sem("ld_" + n) for n in ("wkq", "bq", "bk", "ctx0", "ctx1", "ctx2", "wo", "wv", "bvo", "gates",
                                          "x0", "x1", "w1", "w2", "wg")}
        s_ident0 = sem("ident_zero"); s_ident = sem("ident_ready")
        s_const = sem("constants_ready")
        s_gate = sem("gate_tanh_ready"); s_fscale = sem("ffn_scale_ready")
        s_warm = sem("warm_up_operand_ready")
        s_wide = sem("wide_biases_ready")
        s_wkq_mm = sem("wkq_product"); s_wkq_hi = sem("wkq_hi_ready"); s_wkq_lo = sem("wkq_lo_ready")
        s_small_mm = sem("small_products"); s_small = sem("small_ready")
        s_bqwk_mm = sem("bqwk_transposed"); s_bqwk = sem("bqwk_row_ready"); s_kbcol = sem("key_bias_column_ready")
        s_cT = sem("ctx_transposed"); s_cT_hi = sem("ctxT_hi_ready"); s_cT_lo = sem("ctxT_lo_ready")
        s_pad = sem("ctxT_pad_zero")
        s_kq_mm = sem("KQ_product"); s_kq_hi = sem("KQ_hi_ready"); s_kq_lo = sem("KQ_lo_ready")
        s_kb_mm = sem("key_bias_transposed"); s_kb = sem("key_bias_ready")
        s_woT_mm = sem("wo_transposed"); s_woT = sem("woT_ready"); s_woT_hi = sem("woT_hi_ready")
        s_woT_lo = sem("woT_lo_ready")
        s_wvo_mm = sem("wvo_product"); s_wvo_hi = sem("wvo_hi_ready"); s_wvo_lo = sem("wvo_lo_ready")
        s_vb_mm = sem("vo_bias_product"); s_vb = sem("vo_bias_ready")
        s_vo_mm = sem("VO_product"); s_vo_sum = sem("VO_sum_ready"); s_vo_hi = sem("VO_hi_ready")
        s_vo_lo = sem("VO_lo_ready")
        s_xbn = sem("x_bn_ready"); s_xmv = sem("x_mv_ready"); s_xve = sem("x_ve_ready")
        s_xpow = sem("x_rstd_ready"); s_xsh = sem("x_shift_ready")
        s_xn = sem("xn_ready"); s_xnT = sem("xn_transposed"); s_xnT_hi = sem("xnT_hi_ready")
        s_xnT_lo = sem("xnT_lo_ready")
        s_score = sem("scores_product"); s_biased = sem("scores_biased"); s_max = sem("row_max_ready")
        s_ebias = sem("exp_bias_ready"); s_exp = sem("probs_ready")
        s_pT = sem("probs_transposed"); s_pT_hi = sem("pT_hi_ready"); s_pT_lo = sem("pT_lo_ready")
        s_sum = sem("row_sum_ready"); s_inv = sem("row_inv_ready"); s_gain = sem("row_gain_ready")
        s_attn = sem("attention_product"); s_proj = sem("last_projection"); s_resid = sem("resid_ready"); s_x1 = sem("x1_ready")
        s_zbn = sem("z_bn_ready"); s_zmv = sem("z_mv_ready"); s_zall = sem("z_statistics_kept")
        s_w1T_mm = sem("w1_transposed"); s_w1T_hi = sem("w1T_hi_ready"); s_w1T_lo = sem("w1T_lo_ready")
        s_wgT_mm = sem("wg_transposed"); s_wgT_hi = sem("wgT_hi_ready"); s_wgT_lo = sem("wgT_lo_ready")
        s_w2T_mm = sem("w2_transposed"); s_w2T_hi = sem("w2T_hi_ready"); s_w2T_lo = sem("w2T_lo_ready")
        s_zve = sem("z_ve_ready"); s_zpow = sem("z_rstd_ready"); s_zneg = sem("z_negm_ready")
        s_zsh = sem("z_shift_ready")
        s_z = sem("z_ready"); s_zT = sem("z_transposed"); s_zT_hi = sem("zT_hi_ready")
        s_zT_lo = sem("zT_lo_ready")
        s_up = sem("up_product"); s_logit2 = sem("first_logits_ready"); s_logit = sem("last_logits_ready"); s_top = sem("top8_ready")
        s_idx = sem("top_idx_ready"); s_diff = sem("top_diff_ready"); s_ttanh = sem("top_tanh_ready")
        s_tgate = sem("top_gate_ready"); s_is = sem("is_top_ready"); s_two = sem("gate_two_ready")
        s_eg = sem("expert_gate_ready")
        s_gelu = sem("gelu_ready"); s_gated = sem("hidden_gated"); s_gated2 = sem("second_half_gated")
        s_hT = sem("hidden_transposed"); s_hT_hi = sem("hT_hi_ready"); s_hT_lo = sem("hT_lo_ready")
        s_down = sem("down_product"); s_final = sem("final_ready"); s_out = sem("out_stored")

        def f32(ap):
            return ap.bitcast(F32)

        def count(eng, value):
            return value if isinstance(value, int) else eng.compute_val(value)

        def tile_of(t):
            return X[:, bass.ds(t * D, D)]

        def projected(last):
            return (S[3] if last else A)[:, D:2 * D]

        def VO_bank(n):
            return (A, T[0], T[1])[n % 3]

        def key_rows(n):
            return P if n < FULL else REST

        def ctx_bank(g):
            return (*S, S[0], S[1], B)[g]

        def ctxT_part(dst, g):
            n = 2 * P if g < 6 else REST
            return (dst[:, :, g * 2 * P:g * 2 * P + n],
                    ctx_bank(g)[:].rearrange("p (a k) -> p a k", a=2)[:, :, 0:n])

        def pT_part(dst, g):
            tiles = GROUPS[g]
            rows = key_rows(tiles[-1])
            n = len(tiles)
            return (rows, dst[0:rows, tiles[0]:tiles[0] + n, :].rearrange("p a d -> p (a d)"),
                    T[g % 2][0:rows, 0:n * P])

        def gated_half(t, h):
            half = slice(h * E // 2, (h + 1) * E // 2)
            units = hid[:, t % 2, half]
            return units, units, expert_gate[:, t % 2, half].unsqueeze(2).to_broadcast([P, E // 2, R])

        def wgT_part():
            return B[:, 0:DC * E].rearrange("p (a b n) -> p a b n", a=DC, b=2)

        block = ctx.enter_context(nc.Block())

        x_rows = x[0].rearrange("(p t) d -> p (t d)", t=TILES)
        out_rows = out[0].rearrange("(p t) d -> p (t d)", t=TILES)

        def column(v):
            return v.rearrange("(a p) -> p a", p=P)

        def row(v):
            return v.rearrange("(a d) -> a d", a=1)

        @block.sync
        def _(sp):
            full = ctx_1024[0, 0:FULL * P, :].rearrange("(p n) d -> p n d", n=FULL)
            third = FULL // 3
            for n in range(0, third, 2):
                sp.dma_start(ctx_nat[:, n:n + 2, :], full[:, n:n + 2, :]).then_inc(ld["ctx0"], 16)
            sp.dma_start(wk[:], Wk.rearrange("(a p) d -> p a d", p=P)).then_inc(ld["wkq"], 16)
            sp.dma_start(wq[:, :, 0:D], Wq.rearrange("(a p) d -> p a d", p=P)).then_inc(ld["wkq"], 16)
            sp.dma_start(ctx_nat[:, third:2 * third, :], full[:, third:2 * third, :]).then_inc(ld["ctx1"], 16)
            sp.dma_start(ctx_nat[:, 2 * third:FULL, :], full[:, 2 * third:FULL, :]).then_inc(ld["ctx2"], 16)
            sp.dma_start(ctx_nat[0:REST, FULL, :], ctx_1024[0, FULL * P:KEYS, :]).then_inc(ld["ctx2"], 16)
            sp.dma_start(wo[:], Wo.rearrange("(a p) d -> p a d", p=P)).then_inc(ld["wo"], 16)
            sp.dma_start(wv[:], Wv.rearrange("(a p) d -> p a d", p=P)).then_inc(ld["wv"], 16)
            n = TILES // 2 * D
            with nc.allow_non_contiguous_dma(reason="short vectors"):
                sp.dma_start(bv_col[:], column(bv)).then_inc(ld["bvo"], 16)
                sp.dma_start(bo_row[:], row(bo)).then_inc(ld["bvo"], 16)
                sp.dma_start(X[:, 0:n], x_rows[:, 0:n]).then_inc(ld["x0"], 16)
                for i, g in enumerate((g_xattn, g_ffn)):
                    sp.dma_start(gates[:, i:i + 1], row(g).to_broadcast([P, 1])).then_inc(ld["gates"], 16)
                sp.dma_start(X[:, n:2 * n], x_rows[:, n:2 * n]).then_inc(ld["x1"], 16)
                sp.dma_start(wg[:], Wg).then_inc(ld["wg"], 16)
                sp.dma_start(bg_wide[:], row(bg).to_broadcast([P, E])).then_inc(ld["wg"], 16)
            sp.dma_start(w1[:], W1.rearrange("e r d -> (e r) d").rearrange("(a p) d -> p a d", p=P)
                         ).then_inc(ld["w1"], 16)
            for dc in range(DC):
                sp.dma_start(w2[:, dc, :, :], W2[:, dc * P:(dc + 1) * P, :].rearrange("e p r -> p e r")
                             ).then_inc(ld["w2"], 16)
            for t in range(0, TILES - 2, 2):
                sp.wait_ge(s_final, t + 2)
                sp.dma_start(out_rows[:, t * D:(t + 2) * D], X[:, t * D:(t + 2) * D]).then_inc(s_out, 16)
            for t in range(TILES - 2, TILES):
                sp.wait_ge(s_final, t + 1)
                sp.dma_start(out_rows[:, t * D:(t + 1) * D], X[:, t * D:(t + 1) * D]).then_inc(s_out, 16)
            sp.wait_ge(s_out, 16 * (TILES // 2 + 1))

        @block.gpsimd
        def _(pool):
            pool.memset(ident[:], 0.0).then_inc(s_ident0, 1)
            pool.wait_ge(s_ident0, 1)
            pool.affine_select(out=ident[:], in_=ident[:], compare_op=ALU.not_equal, fill=1.0, base=0,
                               pattern=[[-1, P]], channel_multiplier=1).then_inc(s_ident, 1)
            pool.memset(minus_half[:], -0.5).then_inc(s_const, 1)
            for e in range(E):
                pool.memset(expert_no[:, e:e + 1], float(e)).then_inc(s_const, 1)
            pool.memset(half_signs[:, 0:1], 0.5).then_inc(s_const, 1)
            pool.memset(half_signs[:, 1:2], -0.5).then_inc(s_const, 1)
            pool.memset(halves[:], 0.5).then_inc(s_const, 1)
            pool.memset(ones_row[:], 1.0).then_inc(s_const, 1)
            pool.wait_ge(s_const, E + 5)

            def x_moments(t, par):
                now, before = count(pool, t + 1), count(pool, t - 1)
                pool.wait_ge(s_const, E + 5)
                pool.wait_ge(s_xmv, now)
                if not isinstance(t, int) or t >= 2:
                    pool.wait_ge(s_xn, before)
                pool.tensor_scalar(x_ve[:, par:par + 1], x_mv[:, par, 1:2], EPS, None, ALU.add).then_inc(s_xve, 1)
                pool.wait_ge(s_xve, t + 1)
                pool.tensor_tensor(x_rstd[:, par:par + 1], x_ve[:, par:par + 1], minus_half[:, 0:1],
                                   ALU.pow).then_inc(s_xpow, 1)
                pool.wait_ge(s_const, E + 5)
                pool.wait_ge(s_xpow, now)
                pool.tensor_scalar(x_shift[:, par:par + 1], x_mv[:, par, 0:1], x_rstd[:, par:par + 1], -1.0,
                                   ALU.mult, ALU.mult).then_inc(s_xsh, 1)

            def vo_low(n):
                k = key_rows(n)
                pool.wait_ge(s_vo_hi, n + 1)
                pool.tensor_tensor(VO_lo[0:k, n, :], VO_sum[0:k, n % 3, :], f32(VO_hi[0:k, n, :]),
                                   ALU.subtract).then_inc(s_vo_lo, 1)

            for t in range(2):
                x_moments(t, t % 2)
            for n in range(KT):
                vo_low(n)
                if n == 9:
                    x_moments(2, 0)

            def keep_z(t, par):
                pool.wait_ge(s_const, E + 5)
                pool.wait_ge(s_zmv, t + 1)
                pool.tensor_copy(z_all[:, bass.ds(t * 2, 2)], z_mv[:, par, :]).then_inc(s_zall, 1)

            x_moments(3, 1)
            with pool.Fori(0, TILES - 5, 2) as t:
                keep_z(t, 0)
                x_moments(t + 4, 0)
                keep_z(t + 1, 1)
                x_moments(t + 5, 1)

            def z_moments(t0, t1):
                batch = 1 if t0 == 0 else 2
                mean, var = (z_all[:].rearrange("p (t k) -> p t k", k=2)[:, t0:t1, k] for k in (0, 1))
                pool.wait_ge(s_zall, t1)
                pool.tensor_scalar(z_ve[:, t0:t1], var, EPS, None, ALU.add).then_inc(s_zve, 1)
                pool.wait_ge(s_zve, batch)
                pool.tensor_tensor(z_rstd[:, t0:t1], z_ve[:, t0:t1], minus_half[:, t0:t1], ALU.pow
                                   ).then_inc(s_zpow, 1)
                pool.tensor_scalar(z_negm[:, t0:t1], mean, -1.0, None, ALU.mult).then_inc(s_zneg, 1)
                pool.wait_ge(s_zneg, batch)
                pool.wait_ge(s_zpow, batch)
                pool.tensor_tensor(z_shift[:, t0:t1], z_negm[:, t0:t1], z_rstd[:, t0:t1], ALU.mult
                                   ).then_inc(s_zsh, 1)

            for t in range(TILES - 4, TILES - 2):
                keep_z(t, t % 2)
            z_moments(0, TILES - 2)
            keep_z(TILES - 2, 0)

            def gate_hidden(t, par):
                pool.wait_ge(s_gelu, t + 1)
                pool.wait_ge(s_eg, t + 1)
                pool.tensor_tensor(hid[:, par], hid[:, par],
                                   expert_gate[:, par, :].unsqueeze(2).to_broadcast([P, E, R]),
                                   ALU.mult).then_inc(s_gated, 1)

            gate_hidden(0, 0)
            gate_hidden(1, 1)
            gate_hidden(2, 0)
            keep_z(TILES - 1, 1)
            z_moments(TILES - 2, TILES)
            gate_hidden(3, 1)
            with pool.Fori(4, TILES - 3, 2) as t:
                gate_hidden(t, 0)
                gate_hidden(t + 1, 1)
            for t in range(TILES - 2, TILES):
                pool.wait_ge(s_gelu, t + 1)
                pool.wait_ge(s_eg, t + 1)
                pool.tensor_tensor(*gated_half(t, 0), ALU.mult).then_inc(s_gated, 1)

        @block.tensor
        def _(pe):
            def three(dst, lhs_hi, lhs_lo, rhs_hi, rhs_lo, first, last):
                pe.matmul(dst, lhs_hi, rhs_hi, start=first, stop=False)
                pe.matmul(dst, lhs_hi, rhs_lo, start=False, stop=False)
                return pe.matmul(dst, lhs_lo, rhs_hi, start=False, stop=last)

            def transpose_ctx(g):
                piece, count_of = ((("ctx0", 32),) * 2 + (("ctx1", 16),) * 2 + (("ctx2", 32),) * 3)[g]
                pe.wait_ge(ld[piece], count_of)
                if g in (4, 5):
                    pe.wait_ge(s_cT_lo, g - 3)
                for jc in range(DC):
                    for n in [n for n in (2 * g, 2 * g + 1) if n < KT]:
                        k = key_rows(n)
                        at = jc * 2 * P + (n - 2 * g) * P
                        mm = pe.transpose(ctx_bank(g)[:, at:at + k], ctx_nat[0:k, n, jc * P:(jc + 1) * P],
                                          ident[0:k, 0:k])
                mm.then_inc(s_cT, 1)

            pe.wait_ge(s_warm, 1)
            for _ in range(WARM_UP):
                pe.matmul(A[:, 0:P], warm[:], warm[:], start=True, stop=True)
            pe.wait_ge(s_ident, 1)
            transpose_ctx(0)
            transpose_ctx(1)
            pe.wait_ge(ld["wkq"], 32)
            pe.wait_ge(ld["bq"], 16)
            for jc in range(DC):
                for cc in range(DC):
                    mm = pe.matmul(T[jc][:, 0:D + 1], wk[:, cc, jc * P:(jc + 1) * P], wq[:, cc, :],
                                   start=(cc == 0), stop=(cc == DC - 1))
                mm.then_inc(s_wkq_mm, 1)
            for g in range(2, 7):
                transpose_ctx(g)
            pe.wait_ge(ld["bk"], 16)
            pe.wait_ge(s_wide, 1)
            for i in range(DC + 1):
                for cc in range(DC):
                    w = wq[:, cc, i * P:(i + 1) * P] if i < DC else bq_wide[:, cc, :]
                    mm = pe.matmul(A[:, i:i + 1], w, bk_col[:, cc:cc + 1], start=(cc == 0), stop=(cc == DC - 1))
            mm.then_inc(s_small_mm, 1)
            pe.wait_ge(s_small, 2)
            pe.wait_ge(s_wkq_lo, 2)
            for jc in range(DC):
                mm = pe.transpose(T[1][:, jc * P:(jc + 1) * P], small[:, 3 + jc:4 + jc].to_broadcast([P, P]), ident[:])
            mm.then_inc(s_bqwk_mm, 1)
            def transpose_wo():
                pe.wait_ge(ld["wo"], 16)
                pe.wait_ge(s_wkq_lo, 2)
                pe.wait_ge(s_small, 2)
                for cc in range(DC):
                    for oc in range(DC):
                        mm = pe.transpose(T[0][:, cc * D + oc * P:cc * D + (oc + 1) * P],
                                          wo[:, oc, cc * P:(cc + 1) * P], ident[:])
                mm.then_inc(s_woT_mm, 1)

            pe.wait_ge(s_wkq_hi, 2)
            pe.wait_ge(s_wkq_lo, 2)
            for u in range(DC * 4):
                fc, (k0, kn) = u // 4, CHUNKS[u % 4]
                if u < 4:
                    groups = -(-min(k0 + kn, KEYS) // (2 * P))
                    pe.wait_ge(s_cT_hi, groups)
                    pe.wait_ge(s_cT_lo, max(groups, (5, 6)[u] if u < 2 else 0))
                else:
                    pe.wait_ge(s_kq_lo, u - 3)
                if u == 3:
                    pe.wait_ge(s_pad, 2)
                for jc in range(DC):
                    mm = three(S[u % 4][:, 0:kn], wkq_hi[:, jc, fc * P:(fc + 1) * P],
                               wkq_lo[:, jc, fc * P:(fc + 1) * P], ctxT_hi[:, jc, k0:k0 + kn],
                               ctxT_lo[:, jc, k0:k0 + kn], jc == 0, jc == DC - 1)
                mm.then_inc(s_kq_mm, 1)
                if u == 0:
                    transpose_wo()
            def transpose_xn(t, par):
                pe.wait_ge(s_xn, t + 1)
                if not isinstance(t, int) or t >= 1:
                    pe.wait_ge(s_xnT_lo, t)
                for dc in range(DC):
                    mm = pe.transpose(B[:, dc * P:(dc + 1) * P], xn[:, par, dc * P:(dc + 1) * P], ident[:])
                mm.then_inc(s_xnT, 1)

            transpose_xn(0, 0)
            pe.wait_ge(s_woT, 1)
            pe.wait_ge(s_bqwk, 1)
            pe.wait_ge(ld["wv"], 16)
            for jc in range(DC):
                for cc in range(DC):
                    mm = pe.matmul(T[1][:, jc * D:(jc + 1) * D], wv[:, cc, jc * P:(jc + 1) * P], woT[:, cc, :],
                                   start=(cc == 0), stop=(cc == DC - 1))
            mm.then_inc(s_wvo_mm, 1)
            pe.wait_ge(ld["bvo"], 32)
            pe.wait_ge(s_wide, 2)
            pe.wait_ge(s_const, E + 5)
            pe.wait_ge(s_small, 3)
            for cc in range(DC):
                pe.matmul(A[:, 0:D], bv_wide[:, cc, :], woT[:, cc, :], start=(cc == 0), stop=False)
            pe.matmul(A[:, 0:D], ones_row[:], bo_row[:], start=False, stop=True).then_inc(s_vb_mm, 1)
            for g in range(4):
                pe.wait_ge(s_kq_lo, 5 + g)
                for n in GROUPS[g]:
                    pe.wait_ge(s_kbcol, n + 1)
                    k, at = key_rows(n), (n % 4) * P
                    mm = pe.transpose(S[g][:, at:at + k], kb_col[0:k, n:n + 1].to_broadcast([k, P]), ident[0:k, 0:k])
                mm.then_inc(s_kb_mm, 1)

            def turn(t, par, g, first=False):
                if g < 2:
                    pe.wait_ge(s_exp, t * 2 + (g + 1))
                if first and g < 2:
                    pe.wait_ge(s_vo_sum, KT - 2 + g)
                if not (first and g < 2):
                    pe.wait_ge(s_pT_lo, t * 4 + (g - 1))
                for n in GROUPS[g]:
                    k, at = key_rows(n), (n % 4) * P
                    mm = pe.transpose(T[g % 2][0:k, at:at + P], probs[:, par, n * P:n * P + k], ident[:])
                mm.then_inc(s_pT, 1)

            def scores(t, par, first=False, turns=True):
                pe.wait_ge(s_xnT_hi, t + 1)
                pe.wait_ge(s_xnT_lo, t + 1)
                if isinstance(t, int) and t == 1:
                    pe.wait_ge(s_w1T_lo, 2)
                    pe.wait_ge(s_w2T_lo, 2)
                for c, (k0, kn) in enumerate(CHUNKS):
                    if first:
                        pe.wait_ge(s_kb, c + 1)
                    else:
                        pe.wait_ge(s_biased, t * 4 + (c - 3))
                    for dc in range(DC):
                        mm = three(S[c][:, 0:kn], xnT_hi[:, par, dc, :], xnT_lo[:, par, dc, :],
                                   KQ_hi[:, dc, k0:k0 + kn], KQ_lo[:, dc, k0:k0 + kn], dc == 0, dc == DC - 1)
                    mm.then_inc(s_score, 1)
                    if not first:
                        turn(t - 1, 1 - par, c, first=isinstance(t, int) and t == 1)

            def project(t, par, first=False, last=False):
                if first:
                    pe.wait_ge(s_vo_sum, KT)
                elif last:
                    pe.wait_ge(s_biased, TILES * 4)
                else:
                    pe.wait_ge(s_x1, t)
                for dc in range(DC):
                    mm = three(projected(last), xnT_hi[:, par, dc, :], xnT_lo[:, par, dc, :],
                               woT_hi[:, dc, :], woT_lo[:, dc, :], dc == 0, dc == DC - 1)
                if last:
                    mm.then_inc(s_proj, 1)

            def weigh(t, g):
                pe.wait_ge(s_pT_hi, t * 4 + (g + 1))
                pe.wait_ge(s_pT_lo, t * 4 + (g + 1))
                for n in GROUPS[g]:
                    k = key_rows(n)
                    mm = three(A[:, 0:D], pT_hi[0:k, n, :], pT_lo[0:k, n, :], VO_hi[0:k, n, :],
                               VO_lo[0:k, n, :], n == 0, n == KT - 1)
                if g == 3:
                    mm.then_inc(s_attn, 1)

            def attend(t, par, first=False, ahead=True):
                project(t, par, first)
                if first:
                    pe.wait_ge(s_wgT_lo, 1)
                if ahead:
                    transpose_xn(t + 2, par)
                for g in range(4):
                    if first:
                        pe.wait_ge(s_vo_lo, GROUPS[g][-1] + 1)
                    weigh(t, g)

            pe.wait_ge(s_kq_hi, 8)
            scores(0, 0, first=True)
            transpose_xn(1, 1)
            def transpose_w1():
                pe.wait_ge(ld["w1"], 16)
                pe.wait_ge(s_biased, 2)
                for dc in range(DC):
                    for et in range(ET):
                        mm = pe.transpose(S[dc][:, et * P:(et + 1) * P], w1[:, et, dc * P:(dc + 1) * P], ident[:])
                    mm.then_inc(s_w1T_mm, 1)

            def transpose_w2():
                pe.wait_ge(ld["w2"], 16 * DC)
                pe.wait_ge(s_biased, 4)
                for b in range(2):
                    for et in (2 * b, 2 * b + 1):
                        for dc in range(DC):
                            at = (et % 2) * D + dc * P
                            mm = pe.transpose(S[2 + b][:, at:at + P],
                                              w2[:, dc].rearrange("p e r -> p (e r)")[:, et * P:(et + 1) * P], ident[:])
                    mm.then_inc(s_w2T_mm, 1)

            def transpose_wg():
                pe.wait_ge(ld["wg"], 32)
                pe.wait_ge(s_xnT_lo, 2)
                for dc in range(DC):
                    mm = pe.transpose(B[:, dc * E:(dc + 1) * E], wg[:, dc * P:(dc + 1) * P], ident[0:E, 0:E])
                mm.then_inc(s_wgT_mm, 1)

            pe.wait_ge(s_wvo_hi, 1)
            pe.wait_ge(s_wvo_lo, 1)
            pe.wait_ge(s_woT_lo, 1)
            pe.wait_ge(s_vb, 1)
            for n in range(KT):
                k = key_rows(n)
                if n >= 3:
                    pe.wait_ge(s_vo_sum, n - 2)
                for jc in range(DC):
                    mm = three(VO_bank(n)[0:k, 0:D], ctxT_hi[:, jc, n * P:n * P + k],
                               ctxT_lo[:, jc, n * P:n * P + k], wvo_hi[:, jc, :], wvo_lo[:, jc, :],
                               jc == 0, jc == DC - 1)
                mm.then_inc(s_vo_mm, 1)
                if n == 2:
                    transpose_w1()
                elif n == 5:
                    transpose_w2()
                elif n == 8:
                    transpose_wg()

            pe.wait_ge(s_woT_hi, 1)
            for t in range(2):
                scores(t + 1, (t + 1) % 2)
                attend(t, t % 2, first=(t == 0))
            with pe.Fori(2, TILES - 3, 2) as t:
                for h in range(2):
                    scores(t + (h + 1), 1 - h)
                    attend(t + h, h)
            scores(TILES - 1, 1)
            def transpose_z(t, par, first=False):
                pe.wait_ge(s_z, t + 1)
                pe.wait_ge(s_xnT_lo, TILES) if first else pe.wait_ge(s_zT_lo, t)
                for dc in range(DC):
                    mm = pe.transpose(B[:, dc * P:(dc + 1) * P], zb[:, par, dc * P:(dc + 1) * P], ident[:])
                mm.then_inc(s_zT, 1)

            def up(t, par, first=False):
                pe.wait_ge(s_zT_hi, t + 1)
                pe.wait_ge(s_zT_lo, t + 1)
                if not first:
                    pe.wait_ge(s_gelu, t - 1)
                for b in range(2):
                    for dc in range(DC):
                        mm = three(S[2 * par + b][:, 0:UPW], zT_hi[:, par, dc, :], zT_lo[:, par, dc, :],
                                   w1T_hi[:, dc, b, :], w1T_lo[:, dc, b, :], dc == 0, dc == DC - 1)
                mm.then_inc(s_up, 1)

            def transpose_hidden(t, par, first=False):
                pe.wait_ge(s_gated, t + 1)
                if not first:
                    pe.wait_ge(s_hT_lo, t - 1)
                flat = hid[:, par].rearrange("p e r -> p (e r)")
                for et in range(ET):
                    mm = pe.transpose(T[par][:, et * P:(et + 1) * P], flat[:, et * P:(et + 1) * P], ident[:])
                mm.then_inc(s_hT, 1)

            def down(t, par, bank=A, bank_free=None):
                pe.wait_ge(s_hT_hi, t + 1)
                pe.wait_ge(s_hT_lo, t + 1)
                pe.wait_ge(*(bank_free or (s_final, t)))
                for et in range(ET):
                    mm = three(bank[:, 0:D], hT_hi[:, par, et, :], hT_lo[:, par, et, :],
                               w2T_hi[:, et, :], w2T_lo[:, et, :], et == 0, et == ET - 1)
                mm.then_inc(s_down, 1)

            last = TILES - 1
            project(last - 1, 0)
            weigh(last - 1, 0)
            weigh(last - 1, 1)
            turn(last, 1, 0)
            weigh(last - 1, 2)
            transpose_z(0, 0, first=True)
            turn(last, 1, 1)
            weigh(last - 1, 3)
            turn(last, 1, 2)
            project(last, 1, last=True)
            turn(last, 1, 3)
            pe.wait_ge(s_w1T_hi, 2)
            pe.wait_ge(s_w1T_lo, 2)
            pe.wait_ge(s_wgT_hi, 1)
            up(0, 0, first=True)
            transpose_z(1, 1)
            pe.wait_ge(s_x1, last)
            weigh(last, 0)
            weigh(last, 1)
            pe.wait_ge(s_resid, TILES)
            up(1, 1, first=True)
            transpose_z(2, 0)
            weigh(last, 2)
            weigh(last, 3)
            transpose_hidden(0, 0, first=True)
            pe.wait_ge(s_w2T_hi, 2)
            pe.wait_ge(s_w2T_lo, 2)
            up(2, 0)
            transpose_z(3, 1)
            transpose_hidden(1, 1, first=True)
            down(0, 0, bank_free=(s_x1, TILES))
            up(3, 1)
            transpose_z(4, 0)
            transpose_hidden(2, 0)
            down(1, 1)
            with pe.Fori(4, TILES - 3, 2) as u:
                for h in range(2):
                    up(u + h, h)
                    transpose_z(u + (h + 1), 1 - h)
                    transpose_hidden(u + (h - 1), 1 - h)
                    down(u + (h - 2), h)
            transpose_z(last, 1)
            up(last - 1, 0)
            transpose_hidden(last - 2, 1)
            up(last, 1)
            down(last - 3, 0)
            pe.wait_ge(s_gated2, 1)
            transpose_hidden(last - 1, 0)
            down(last - 2, 1, B, (s_zT_lo, TILES))
            down(last - 1, 0, A, (s_final, last - 2))
            pe.wait_ge(s_gated, TILES)
            pe.wait_ge(s_gated2, 2)
            pe.wait_ge(s_hT_lo, last)
            flat = hid[:, 1].rearrange("p e r -> p (e r)")
            for et in range(ET):
                mm = pe.transpose(T[et // 2][:, (et % 2) * P:(et % 2 + 1) * P], flat[:, et * P:(et + 1) * P], ident[:])
                if et % 2 == 1:
                    mm.then_inc(s_hT, 1)
            for h in range(2):
                pair = range(2 * h, 2 * h + 2)
                pe.wait_ge(s_hT_hi, TILES + h)
                if h == 0:
                    pe.wait_ge(s_final, last - 1)
                for et in pair:
                    pe.matmul(B[:, 0:D], hT_hi[:, 1, et, :], w2T_hi[:, et, :], start=(et == 0), stop=False)
                    pe.matmul(B[:, 0:D], hT_hi[:, 1, et, :], w2T_lo[:, et, :], start=False, stop=False)
                pe.wait_ge(s_hT_lo, TILES + h)
                for et in pair:
                    mm = pe.matmul(B[:, 0:D], hT_lo[:, 1, et, :], w2T_hi[:, et, :], start=False, stop=(et == ET - 1))
            mm.then_inc(s_down, 1)

        @block.scalar
        def _(act):
            with nc.allow_non_contiguous_dma(reason="short vectors"):
                act.dma_start(wq[:, :, D], column(bq)).then_inc(ld["bq"], 16)
                act.dma_start(bk_col[:], column(bk)).then_inc(ld["bk"], 16)
            act.preload_act_table(ACT.Exp)

            def ctx_high(g):
                act.wait_ge(s_cT, g + 1)
                act.activation(*ctxT_part(ctxT_hi, g), ACT.Copy).then_inc(s_cT_hi, 1)

            ctx_high(0)
            ctx_high(1)
            for jc in range(DC):
                act.wait_ge(s_wkq_mm, jc + 1)
                act.activation(wkq_hi[:, jc, :], T[jc][:, 0:D], ACT.Copy).then_inc(s_wkq_hi, 1)
            for g in range(2, 7):
                ctx_high(g)
            act.wait_ge(s_bqwk_mm, 1)
            act.activation(bqwk_row[:], T[1][:, 0:D], ACT.Copy).then_inc(s_bqwk, 1)
            flat = lambda w: w[:].rearrange("p a d -> p (a d)")
            def normalize_x(t, par):
                act.wait_ge(s_xsh, t + 1)
                if not isinstance(t, int) or t >= 2:
                    act.wait_ge(s_xnT, t - 1)
                act.activation(xn[:, par, :], tile_of(t), ACT.Identity, bias=x_shift[:, par:par + 1],
                               scale=x_rstd[:, par:par + 1]).then_inc(s_xn, 1)

            def xnT_high(t, par):
                act.wait_ge(s_xnT, t + 1)
                act.activation(xnT_hi[:, par].rearrange("p a d -> p (a d)"), B[:, 0:D], ACT.Copy
                               ).then_inc(s_xnT_hi, 1)

            act.wait_ge(s_small, 3)
            for u in range(DC * 4):
                fc, (k0, kn) = u // 4, CHUNKS[u % 4]
                act.wait_ge(s_kq_mm, u + 1)
                act.activation(KQ_hi[:, fc, k0:k0 + kn], S[u % 4][:, 0:kn], ACT.Identity,
                               bias=small[:, fc:fc + 1]).then_inc(s_kq_hi, 1)
                if u == 1:
                    act.wait_ge(s_woT_mm, 1)
                    act.activation(flat(woT), T[0][:], ACT.Copy).then_inc(s_woT, 1)
                if u == 3:
                    act.wait_ge(s_woT_mm, 1)
                    act.activation(flat(woT_hi), T[0][:], ACT.Copy).then_inc(s_woT_hi, 1)
                if u == 5:
                    act.wait_ge(ld["x0"], 16)
                    normalize_x(0, 0)
            xnT_high(0, 0)
            normalize_x(1, 1)
            act.wait_ge(s_wvo_mm, 1)
            act.activation(flat(wvo_hi), T[1][:], ACT.Copy).then_inc(s_wvo_hi, 1)
            act.wait_ge(s_vb_mm, 1)
            act.activation(vo_bias[:], A[:, 0:D], ACT.Copy).then_inc(s_vb, 1)
            for g in range(4):
                k0, k1 = g * 4 * P, min((g + 1) * 4 * P, KEYS)
                act.wait_ge(s_kb_mm, g + 1)
                act.activation(key_bias[:, k0:k1], S[g][:, 0:k1 - k0], ACT.Identity, bias=small[:, 2:3]
                               ).then_inc(s_kb, 1)
            act.wait_ge(ld["gates"], 32)
            act.activation(gate_tanh[:], gates[:], ACT.Tanh).then_inc(s_gate, 1)

            def exponentials(t, par, h):
                if h == 0:
                    act.wait_ge(s_ebias, t + 1)
                    if not isinstance(t, int) or t >= 2:
                        act.wait_ge(s_sum, t - 1)
                cut = slice(0, HALF) if h == 0 else slice(HALF, KEYS)
                act.activation(probs[:, par, cut], probs[:, par, cut], ACT.Exp, bias=exp_bias[:, par:par + 1],
                               scale=SCALE, accum_out=half_sum[:, par, h:h + 1]).then_inc(s_exp, 1)

            def pT_high(t, g):
                act.wait_ge(s_pT, t * 4 + (g + 1))
                rows, dst, src = pT_part(pT_hi, g)
                act.activation(dst, src, ACT.Copy).then_inc(s_pT_hi, 1)

            def w1T_high():
                for dc in range(DC):
                    act.wait_ge(s_w1T_mm, dc + 1)
                    act.activation(w1T_hi[:, dc, :, 0:ER // 2], S[dc][:].rearrange("p (b n) -> p b n", b=2), ACT.Copy
                                   ).then_inc(s_w1T_hi, 1)

            def w2T_high():
                for b in range(2):
                    act.wait_ge(s_w2T_mm, b + 1)
                    act.activation(w2T_hi[:, 2 * b:2 * b + 2, :].rearrange("p a d -> p (a d)"), S[2 + b][:],
                                   ACT.Copy).then_inc(s_w2T_hi, 1)

            def wgT_high():
                act.wait_ge(s_wgT_mm, 1)
                act.activation(w1T_hi[:, :, :, ER // 2:UPW], wgT_part(), ACT.Copy).then_inc(s_wgT_hi, 1)

            for n in range(KT):
                k = key_rows(n)
                act.wait_ge(s_vo_sum, n + 1)
                act.activation(VO_hi[0:k, n, :], VO_sum[0:k, n % 3, :], ACT.Copy).then_inc(s_vo_hi, 1)
                if n == 1:
                    xnT_high(1, 1)
                if n in (2, 5, 8):
                    (w1T_high, w2T_high, wgT_high)[n // 3]()
                if n in (3, 7):
                    exponentials(0, 0, n // 7)

            def normalize_z(t, par):
                if not isinstance(t, int) or t >= 2:
                    act.wait_ge(s_zT, t - 1)
                act.activation(zb[:, par, :], tile_of(t), ACT.Identity, bias=z_shift[:, bass.ds(t, 1)],
                               scale=z_rstd[:, bass.ds(t, 1)]).then_inc(s_z, 1)

            def zT_high(t, par):
                act.wait_ge(s_zT, t + 1)
                act.activation(zT_hi[:, par].rearrange("p a d -> p (a d)"), B[:, 0:D], ACT.Copy
                               ).then_inc(s_zT_hi, 1)

            def step(t, par, ahead=True, two_ahead=True):
                pT_high(t, 0)
                if two_ahead:
                    normalize_x(t + 2, par)
                for g in range(1, 4):
                    pT_high(t, g)
                if two_ahead:
                    xnT_high(t + 2, par)
                if ahead:
                    exponentials(t + 1, 1 - par, 0)
                    exponentials(t + 1, 1 - par, 1)

            act.wait_ge(ld["x1"], 16)
            step(0, 0)
            step(1, 1)
            with act.Fori(2, TILES - 3, 2) as t:
                step(t, 0)
                step(t + 1, 1)
            step(TILES - 2, 0, two_ahead=False)
            last = TILES - 1
            act.wait_ge(s_zsh, 1)
            normalize_z(0, 0)
            pT_high(last, 0)
            zT_high(0, 0)
            pT_high(last, 1)
            pT_high(last, 2)
            pT_high(last, 3)
            normalize_z(1, 1)
            act.preload_act_table(ACT.Gelu)

            def gelu(t, par):
                act.wait_ge(s_logit, t + 1)
                if not isinstance(t, int) or t >= 2:
                    act.wait_ge(s_hT, t - 1)
                for b in range(2):
                    ins = act.activation(hid[:, par].rearrange("p (b e) r -> p b (e r)", b=2)[:, b, :],
                                         S[2 * par + b][:, 0:ER // 2], ACT.Gelu)
                    if b == 1:
                        ins.then_inc(s_gelu, 1)

            def gate_of_two(t, par):
                act.wait_ge(s_diff, t + 1)
                act.activation(top_tanh[:, par:par + 1], top_diff[:, par:par + 1], ACT.Tanh, scale=0.5
                               ).then_inc(s_ttanh, 1)

            def hT_high(t, par):
                act.wait_ge(s_hT, t + 1)
                act.activation(hT_hi[:, par].rearrange("p a d -> p (a d)"), T[par][:], ACT.Copy
                               ).then_inc(s_hT_hi, 1)

            def hT_high_half(h):
                act.wait_ge(s_hT, TILES + h)
                act.activation(hT_hi[:, 1, 2 * h:2 * h + 2, :].rearrange("p a d -> p (a d)"), T[h][:, 0:2 * P],
                               ACT.Copy).then_inc(s_hT_hi, 1)

            def step2(u, par, z1=True, hidden=True, z2=True):
                if z1:
                    zT_high(u + 1, 1 - par)
                gelu(u, par)
                gate_of_two(u, par)
                if z2:
                    normalize_z(u + 2, par)
                if hidden:
                    hT_high(u - 1, 1 - par)

            step2(0, 0, hidden=False)
            step2(1, 1)
            step2(2, 0)
            step2(3, 1)
            act.wait_ge(s_zsh, 2)
            with act.Fori(4, TILES - 3, 2) as u:
                step2(u, 0)
                step2(u + 1, 1)
            step2(TILES - 2, 0, z2=False)
            hT_high(TILES - 2, 0)
            step2(TILES - 1, 1, z1=False, hidden=False, z2=False)
            for h in range(2):
                hT_high_half(h)

        @block.vector
        def _(dve):
            dve.memset(warm[:], 1.0).then_inc(s_warm, 1)
            dve.memset(f32(ctxT_hi[:, :, KEYS:KPAD]), 0.0).then_inc(s_pad, 1)
            dve.memset(f32(ctxT_lo[:, :, KEYS:KPAD]), 0.0).then_inc(s_pad, 1)
            dve.wait_ge(ld["bq"], 16)
            dve.tensor_copy(bq_wide[:], wq[:, :, D:D + 1].to_broadcast([P, DC, P])).then_inc(s_wide, 1)

            def ctx_low(g):
                dve.wait_ge(s_cT_hi, g + 1)
                dst, src = ctxT_part(ctxT_lo, g)
                dve.tensor_tensor(dst, src, f32(ctxT_part(ctxT_hi, g)[0]), ALU.subtract).then_inc(s_cT_lo, 1)

            ctx_low(0)
            ctx_low(1)
            for jc in range(DC):
                dve.wait_ge(s_wkq_hi, jc + 1)
                dve.tensor_copy(small[:, 3 + jc:4 + jc], T[jc][:, D:D + 1]).then_inc(s_small, 1)
                dve.tensor_tensor(wkq_lo[:, jc, :], T[jc][:, 0:D], f32(wkq_hi[:, jc, :]), ALU.subtract
                                  ).then_inc(s_wkq_lo, 1)
            for g in range(2, 7):
                ctx_low(g)
            dve.wait_ge(s_small_mm, 1)
            dve.tensor_copy(small[:, 0:3], A[:, 0:3]).then_inc(s_small, 1)

            def key_bias_column(n):
                k = key_rows(n)
                dve.wait_ge(s_bqwk, 1)
                if n >= 2:
                    dve.wait_ge(s_kbcol, n - 1)
                dve.tensor_tensor_reduce(
                    out=bqwk_used[0:k, n % 2, :], in0=ctx_nat[0:k, n, :], in1=bqwk_row[0:k, :], scale=1.0, scalar=0.0,
                    op0=ALU.mult, op1=ALU.add, accum_out=kb_col[0:k, n:n + 1]).then_inc(s_kbcol, 1)

            early = KT - DC * 4 - 2
            for n in range(early):
                key_bias_column(n)
            dve.wait_ge(ld["bvo"], 32)
            dve.tensor_copy(bv_wide[:], bv_col[:].unsqueeze(2).to_broadcast([P, DC, P])).then_inc(s_wide, 1)
            dve.wait_ge(s_small, 3)
            flat = lambda w: w[:].rearrange("p a d -> p (a d)")
            def x_statistics(t, par):
                now, before = count(dve, t + 1), count(dve, t - 1)
                dve.wait_ge(ld["x0"], 16)
                if not isinstance(t, int) or t >= 2:
                    dve.wait_ge(s_xsh, before)
                dve.bn_stats(x_bn[:, par, :], tile_of(t)).then_inc(s_xbn, 1)
                dve.wait_ge(ld["x0"], 16)
                dve.wait_ge(s_xbn, now)
                dve.bn_aggr(x_mv[:, par, :], x_bn[:, par, :]).then_inc(s_xmv, 1)

            def xnT_low(t, par):
                dve.wait_ge(s_xnT_hi, t + 1)
                dst, hi = (w[:, par].rearrange("p a d -> p (a d)") for w in (xnT_lo, xnT_hi))
                dve.tensor_tensor(dst, B[:, 0:D], f32(hi), ALU.subtract).then_inc(s_xnT_lo, 1)

            for u in range(DC * 4):
                fc, (k0, kn) = u // 4, CHUNKS[u % 4]
                dve.wait_ge(s_kq_hi, u + 1)
                dve.scalar_tensor_tensor(out=KQ_lo[:, fc, k0:k0 + kn], in0=S[u % 4][:, 0:kn],
                                         scalar=small[:, fc:fc + 1], in1=f32(KQ_hi[:, fc, k0:k0 + kn]),
                                         op0=ALU.add, op1=ALU.subtract).then_inc(s_kq_lo, 1)
                key_bias_column(u + early)
                if u in (1, 2):
                    x_statistics(u - 1, u - 1)
                if u == 4:
                    dve.wait_ge(s_woT_hi, 1)
                    dve.tensor_tensor(flat(woT_lo), T[0][:], f32(flat(woT_hi)), ALU.subtract).then_inc(s_woT_lo, 1)
            xnT_low(0, 0)
            for n in range(DC * 4 + early, KT):
                key_bias_column(n)
            dve.wait_ge(s_wvo_hi, 1)
            dve.tensor_tensor(flat(wvo_lo), T[1][:], f32(flat(wvo_hi)), ALU.subtract).then_inc(s_wvo_lo, 1)

            def biased(t, par, c):
                if c == 0 and (not isinstance(t, int) or t >= 2):
                    dve.wait_ge(s_pT, t * 4 - 4)
                k0, kn = CHUNKS[c]
                n = min(kn, KEYS - k0)
                now = count(dve, t * 4 + (c + 1))
                dve.wait_ge(s_kb, 4)
                dve.wait_ge(s_score, now)
                dve.tensor_tensor_reduce(
                    out=probs[:, par, k0:k0 + n], in0=S[c][:, 0:n], in1=key_bias[:, k0:k0 + n], scale=1.0,
                    scalar=-3.0e38, op0=ALU.add, op1=ALU.max, accum_out=chunk_max[:, par, c:c + 1]
                ).then_inc(s_biased, 1)

            def maximum(t, par):
                dve.wait_ge(s_biased, t * 4 + 4)
                dve.reduce_max(row_max[:, par:par + 1], chunk_max[:, par, :], AX_X).then_inc(s_max, 1)
                dve.wait_ge(s_max, t + 1)
                dve.tensor_scalar(exp_bias[:, par:par + 1], row_max[:, par:par + 1], -SCALE, None, ALU.mult
                                  ).then_inc(s_ebias, 1)

            def pT_low(t, g):
                dve.wait_ge(s_pT_hi, t * 4 + (g + 1))
                rows, dst, src = pT_part(pT_lo, g)
                dve.tensor_tensor(dst, src, f32(pT_part(pT_hi, g)[1]), ALU.subtract).then_inc(s_pT_lo, 1)

            def row_gains(t, par):
                dve.wait_ge(s_exp, t * 2 + 2)
                if not isinstance(t, int) or t >= 1:
                    dve.wait_ge(s_inv, t)
                dve.tensor_tensor(row_sum[:], half_sum[:, par, 0:1], half_sum[:, par, 1:2], ALU.add
                                  ).then_inc(s_sum, 1)
                dve.wait_ge(s_sum, t + 1)
                if not isinstance(t, int) or t >= 1:
                    dve.wait_ge(s_gain, t)
                dve.reciprocal(row_inv[:], row_sum[:]).then_inc(s_inv, 1)
                dve.wait_ge(s_inv, t + 1)
                if not isinstance(t, int) or t >= 1:
                    dve.wait_ge(s_x1, t)
                dve.tensor_scalar(row_gain[:], row_inv[:], gate_tanh[:, 0:1], None, ALU.mult).then_inc(s_gain, 1)

            def residual(t, last=False):
                if last:
                    dve.wait_ge(s_proj, 1)
                    dve.wait_ge(s_x1, t)
                else:
                    dve.wait_ge(s_attn, t + 1)
                dve.scalar_tensor_tensor(out=resid[:], in0=projected(last), scalar=gate_tanh[:, 0:1], in1=tile_of(t),
                                         op0=ALU.mult, op1=ALU.add).then_inc(s_resid, 1)

            def attention_out(t, last=False):
                if last:
                    dve.wait_ge(s_attn, t + 1)
                else:
                    residual(t)
                dve.wait_ge(s_resid, t + 1)
                dve.wait_ge(s_gain, t + 1)
                dve.scalar_tensor_tensor(out=tile_of(t), in0=A[:, 0:D], scalar=row_gain[:], in1=resid[:],
                                         op0=ALU.mult, op1=ALU.add).then_inc(s_x1, 1)

            def z_statistics(t, par):
                dve.wait_ge(ld["x1"], 16)
                dve.wait_ge(s_x1, t + 1)
                if not isinstance(t, int) or t >= 1:
                    dve.wait_ge(s_zmv, t)
                dve.bn_stats(z_bn[:], tile_of(t)).then_inc(s_zbn, 1)
                now, before = count(dve, t + 1), count(dve, t - 1)
                dve.wait_ge(ld["x1"], 16)
                dve.wait_ge(s_zbn, now)
                if not isinstance(t, int) or t >= 2:
                    dve.wait_ge(s_zall, before)
                dve.bn_aggr(z_mv[:, par, :], z_bn[:]).then_inc(s_zmv, 1)

            dve.wait_ge(s_gate, 1)
            dve.tensor_scalar(ffn_scale[:], gate_tanh[:, 1:2], LORA_SCALING, None, ALU.mult).then_inc(s_fscale, 1)
            for c in range(4):
                biased(0, 0, c)
            maximum(0, 0)

            def w1T_low(dc):
                dve.wait_ge(s_w1T_hi, dc + 1)
                dve.tensor_tensor(w1T_lo[:, dc, :, 0:ER // 2], S[dc][:].rearrange("p (b n) -> p b n", b=2),
                                  f32(w1T_hi[:, dc, :, 0:ER // 2]), ALU.subtract).then_inc(s_w1T_lo, 1)

            def w2T_low(b):
                dve.wait_ge(s_w2T_hi, b + 1)
                dst, hi = (w[:, 2 * b:2 * b + 2, :].rearrange("p a d -> p (a d)") for w in (w2T_lo, w2T_hi))
                dve.tensor_tensor(dst, S[2 + b][:], f32(hi), ALU.subtract).then_inc(s_w2T_lo, 1)

            def wgT_low():
                dve.wait_ge(s_wgT_hi, 1)
                dve.tensor_tensor(w1T_lo[:, :, :, ER // 2:UPW], wgT_part(), f32(w1T_hi[:, :, :, ER // 2:UPW]),
                                  ALU.subtract).then_inc(s_wgT_lo, 1)

            dve.wait_ge(s_vb, 1)
            for n in range(KT):
                k = key_rows(n)
                dve.wait_ge(s_vo_mm, n + 1)
                if n >= 3:
                    dve.wait_ge(s_vo_lo, n - 2)
                dve.tensor_tensor(VO_sum[0:k, n % 3, :], VO_bank(n)[0:k, 0:D], vo_bias[0:k, :], ALU.add
                                  ).then_inc(s_vo_sum, 1)
                if n == 1:
                    xnT_low(1, 1)
                if n in (3, 4):
                    w1T_low(n - 3)
                if n in (6, 8):
                    w2T_low(n // 8)
                if n == 9:
                    wgT_low()
                    x_statistics(2, 0)
            dve.wait_ge(ld["x1"], 16)

            def step(t, par, before=True, ahead=True, two_ahead=True, three_ahead=True):
                if before:
                    attention_out(t - 1)
                if ahead:
                    biased(t + 1, 1 - par, 0)
                if before:
                    z_statistics(t - 1, 1 - par)
                pT_low(t, 0)
                if ahead:
                    biased(t + 1, 1 - par, 1)
                row_gains(t, par)
                pT_low(t, 1)
                if ahead:
                    biased(t + 1, 1 - par, 2)
                pT_low(t, 2)
                if three_ahead:
                    x_statistics(t + 3, 1 - par)
                if ahead:
                    biased(t + 1, 1 - par, 3)
                    maximum(t + 1, 1 - par)
                pT_low(t, 3)
                if two_ahead:
                    xnT_low(t + 2, par)

            step(0, 0, before=False)
            step(1, 1)
            with dve.Fori(2, TILES - 5, 2) as t:
                step(t, 0)
                step(t + 1, 1)
            step(TILES - 4, 0)
            step(TILES - 3, 1, three_ahead=False)
            step(TILES - 2, 0, two_ahead=False, three_ahead=False)

            def zT_low(t, par):
                dve.wait_ge(s_zT_hi, t + 1)
                dst, hi = (w[:, par].rearrange("p a d -> p (a d)") for w in (zT_lo, zT_hi))
                dve.tensor_tensor(dst, B[:, 0:D], f32(hi), ALU.subtract).then_inc(s_zT_lo, 1)

            def route(t, par):
                n = E // 2
                dve.wait_ge(s_up, t + 1)
                if not isinstance(t, int) or t >= 2:
                    dve.wait_ge(s_eg, t - 1)
                for b in range(2):
                    ins = dve.tensor_tensor(logits[:, par, b * n:(b + 1) * n], S[2 * par + b][:, ER // 2:UPW],
                                            bg_wide[:, b * n:(b + 1) * n], ALU.add)
                    ins.then_inc(s_logit2 if b == 0 else s_logit, 1)
                dve.wait_ge(ld["wg"], 32)
                dve.wait_ge(s_logit2, t + 1)
                dve.wait_ge(s_logit, t + 1)
                dve.max(top8[:, par, :], logits[:, par, :]).then_inc(s_top, 1)
                dve.wait_ge(ld["wg"], 32)
                dve.wait_ge(s_top, t + 1)
                dve.max_index(top_idx[:, par, :], top8[:, par, :], logits[:, par, :]).then_inc(s_idx, 1)
                dve.tensor_tensor(top_diff[:, par:par + 1], top8[:, par, 0:1], top8[:, par, 1:2], ALU.subtract
                                  ).then_inc(s_diff, 1)

            def spread_gates(t, par):
                dve.wait_ge(s_ttanh, t + 1)
                dve.scalar_tensor_tensor(out=top_gate[:, par, :], in0=half_signs[:], scalar=top_tanh[:, par:par + 1],
                                         in1=halves[:], op0=ALU.mult, op1=ALU.add).then_inc(s_tgate, 1)
                dve.wait_ge(s_idx, t + 1)
                dve.tensor_tensor(is_top[:, par], expert_no[:].unsqueeze(1).to_broadcast([P, 2, E]),
                                  top_idx[:, par, 0:2].unsqueeze(2).to_broadcast([P, 2, E]), ALU.is_equal
                                  ).then_inc(s_is, 1)
                dve.wait_ge(s_tgate, t + 1)
                dve.wait_ge(s_is, t + 1)
                dve.tensor_tensor(gate_two[:, par], is_top[:, par],
                                  top_gate[:, par, :].unsqueeze(2).to_broadcast([P, 2, E]), ALU.mult
                                  ).then_inc(s_two, 1)
                dve.wait_ge(s_two, t + 1)
                if not isinstance(t, int) or t >= 2:
                    dve.wait_ge(s_gated, t - 1)
                dve.tensor_tensor(expert_gate[:, par, :], gate_two[:, par, 0, :], gate_two[:, par, 1, :], ALU.add
                                  ).then_inc(s_eg, 1)

            def hT_low(t, par):
                dve.wait_ge(s_hT_hi, t + 1)
                dst, hi = (w[:, par].rearrange("p a d -> p (a d)") for w in (hT_lo, hT_hi))
                dve.tensor_tensor(dst, T[par][:], f32(hi), ALU.subtract).then_inc(s_hT_lo, 1)

            def finish(t, bank=A):
                dve.wait_ge(s_down, t + 1)
                dve.scalar_tensor_tensor(out=tile_of(t), in0=bank[:, 0:D], scalar=ffn_scale[:], in1=tile_of(t),
                                         op0=ALU.mult, op1=ALU.add).then_inc(s_final, 1)

            dve.wait_ge(s_const, E + 5)
            dve.wait_ge(s_fscale, 1)
            dve.wait_ge(ld["wg"], 32)
            last = TILES - 1
            pT_low(last, 0)
            zT_low(0, 0)
            pT_low(last, 1)
            attention_out(last - 1)
            pT_low(last, 2)
            row_gains(last, 1)
            pT_low(last, 3)
            z_statistics(last - 1, 0)
            residual(last, last=True)

            def step2(u, par, z1=True, hidden=True, last=True):
                route(u, par)
                if z1:
                    zT_low(u + 1, 1 - par)
                spread_gates(u, par)
                if hidden:
                    hT_low(u - 1, 1 - par)
                if last:
                    finish(u - 2)

            zT_low(1, 1)
            step2(0, 0, z1=False, hidden=False, last=False)
            route(1, 1)
            zT_low(2, 0)
            spread_gates(1, 1)
            attention_out(last, last=True)
            z_statistics(last, 1)
            hT_low(0, 0)
            step2(2, 0)
            step2(3, 1)
            with dve.Fori(4, TILES - 3, 2) as u:
                step2(u, 0)
                step2(u + 1, 1)
            def gate_half(t):
                dve.wait_ge(s_gelu, t + 1)
                dve.wait_ge(s_eg, t + 1)
                dve.tensor_tensor(*gated_half(t, 1), ALU.mult).then_inc(s_gated2, 1)

            zT_low(last, 1)
            route(last - 1, 0)
            spread_gates(last - 1, 0)
            gate_half(last - 1)
            hT_low(last - 2, 1)
            finish(last - 3)
            route(last, 1)
            hT_low(last - 1, 0)
            spread_gates(last, 1)
            gate_half(last)
            finish(last - 2, B)
            finish(last - 1)
            for h in range(2):
                dve.wait_ge(s_hT_hi, TILES + h)
                dst, hi = (w[:, 1, 2 * h:2 * h + 2, :].rearrange("p a d -> p (a d)") for w in (hT_lo, hT_hi))
                dve.tensor_tensor(dst, T[h][:, 0:2 * P], f32(hi), ALU.subtract).then_inc(s_hT_lo, 1)
            finish(last, B)


_INS = ["x", "ctx_1024", "g_xattn", "g_ffn", "L0_xattn_Wq", "L0_xattn_bq", "L0_xattn_Wk", "L0_xattn_bk",
        "L0_xattn_Wv", "L0_xattn_bv", "L0_xattn_Wo", "L0_xattn_bo", "L0_ffn_Wg", "L0_ffn_bg", "L0_ffn_W1",
        "L0_ffn_W2"]


def kernel(**inputs):
    import numpy as _np
    import concourse.bacc as _bacc
    from concourse import mybir as _mybir
    from concourse.bass_utils import run_bass_kernel_spmd as _run

    nc = _bacc.Bacc("TRN2", target_bir_lowering=False, num_devices=1)
    arrays, args = {}, []
    for name in _INS:
        a = _np.ascontiguousarray(inputs[name])
        arrays[f"in_{name}"] = a
        args.append(nc.dram_tensor(f"in_{name}", a.shape, _mybir.dt.from_np(a.dtype), kind="ExternalInput").ap())
    shape = tuple(inputs["x"].shape)
    args.append(nc.dram_tensor("out_0", shape, _mybir.dt.float32, kind="ExternalOutput").ap())
    flamingo_layer(nc, *args)
    r = _run(nc, [arrays], core_ids=[0])
    return r.results[0]["out_0"]
```
